# Optimizing a Trainium2 kernel written in Bass

```python
import numpy as np
import jax
import jax.numpy as jnp

def _softmax(x, axis=-1):
    return jax.nn.softmax(x, axis=axis)

def _gelu(x):
    return jax.nn.gelu(x, approximate=True)

def _silu(x):
    return jax.nn.silu(x)

def _sigmoid(x):
    return jax.nn.sigmoid(x)

def _layernorm(x, axis=-1, eps=1e-05):
    m = jnp.mean(x, axis=axis, keepdims=True)
    v = jnp.var(x, axis=axis, keepdims=True)
    return (x - m) / jnp.sqrt(v + eps)

def _scatter_add(tgt, idx, src, axis=0):
    return tgt.at[idx].add(src)

def _segment_sum(src, seg, n):
    return jax.ops.segment_sum(src, seg, n)
kernel_name = 'mk_vit_tower_d1_tok_img256_r4_7624f6'

def setup_inputs(seed: int=0):
    np.random.seed(seed)
    _w = jnp.asarray

    def _rec_inputs():
        import jax
        import jax.numpy as jnp
        _rk = jax.random.key(seed)
        x = 7.22013e-05 + 1.00017 * jax.random.normal(jax.random.fold_in(_rk, 1), (4, 64, 64, 64), jnp.float32)
        return x
    x = _rec_inputs()

    def _L0_tok_setup():
        import jax, jax.numpy as jnp
        import numpy as np
        K = 3
        PAD = (K - 1) // 2
        BN_EPS = 1e-05

        def _unfold(x):
            b, c, h, w = x.shape
            xp = jnp.pad(x, ((0, 0), (0, 0), (PAD, PAD), (PAD, PAD)))
            shifts = [xp[:, :, i:i + h, j:j + w] for i in range(K) for j in range(K)]
            return jnp.stack(shifts, axis=2)
        key = jax.random.key(seed)
        ks = jax.random.split(key, 4)
        b, c, h, w = (8, 64, 64, 64)
        cr = c // 4
        x = jax.random.normal(ks[0], (b, c, h, w), dtype=jnp.float32)
        conv1_w = jax.random.normal(ks[1], (cr, c), dtype=jnp.float32) * (1.0 / np.sqrt(c))
        conv1_b = jnp.zeros((cr,), dtype=jnp.float32)
        bn_gamma = jnp.ones((cr,), dtype=jnp.float32)
        bn_beta = jnp.zeros((cr,), dtype=jnp.float32)
        bn_mean = jnp.zeros((cr,), dtype=jnp.float32)
        bn_var = jnp.ones((cr,), dtype=jnp.float32)
        conv2_w = jax.random.normal(ks[2], (K * K, cr), dtype=jnp.float32) * (1.0 / np.sqrt(cr))
        conv2_b = jnp.zeros((K * K,), dtype=jnp.float32)
        return {'x': x, 'conv1_w': conv1_w, 'conv1_b': conv1_b, 'bn_gamma': bn_gamma, 'bn_beta': bn_beta, 'bn_mean': bn_mean, 'bn_var': bn_var, 'conv2_w': conv2_w, 'conv2_b': conv2_b}
    _L0_tok_all = _L0_tok_setup()
    _L0_tok_in = {k: v for k, v in _L0_tok_all.items() if k in ('conv1_w', 'conv1_b', 'bn_gamma', 'bn_beta', 'bn_mean', 'bn_var', 'conv2_w', 'conv2_b')}
    del _L0_tok_all

    def _L0_attn_setup():
        import jax, jax.numpy as jnp
        import numpy as np
        import math
        B, S, D = (4, 1024, 64)
        key = jax.random.key(seed)
        ks = jax.random.split(key, 9)
        s = 1.0 / math.sqrt(D)
        return {'src': jax.random.normal(ks[0], (B, S, D), dtype=jnp.float32), 'Wq': jax.random.normal(ks[1], (D, D), dtype=jnp.float32) * s, 'bq': jax.random.normal(ks[2], (D,), dtype=jnp.float32) * s, 'Wk': jax.random.normal(ks[3], (D, D), dtype=jnp.float32) * s, 'bk': jax.random.normal(ks[4], (D,), dtype=jnp.float32) * s, 'Wv': jax.random.normal(ks[5], (D, D), dtype=jnp.float32) * s, 'bv': jax.random.normal(ks[6], (D,), dtype=jnp.float32) * s, 'Wo': jax.random.normal(ks[7], (D, D), dtype=jnp.float32) * s, 'bo': jax.random.normal(ks[8], (D,), dtype=jnp.float32) * s}
    _L0_attn_all = _L0_attn_setup()
    _L0_attn_in = {k: v for k, v in _L0_attn_all.items() if k in ('Wq', 'bq', 'Wk', 'bk', 'Wv', 'bv', 'Wo', 'bo')}
    del _L0_attn_all

    def _L0_ffn_setup():
        import math
        import jax, jax.numpy as jnp
        import numpy as np
        CAPACITY_FACTOR = 1.25
        key = jax.random.key(seed)
        ks = jax.random.split(key, 5)
        B, L, D, F, E = (8, 2048, 64, 256, 8)
        h = jax.random.normal(ks[0], (B, L, D), dtype=jnp.float32)
        gate_w = jax.random.normal(ks[1], (D, E), dtype=jnp.float32) * 0.02
        gate_b = jnp.zeros((E,), dtype=jnp.float32)
        w1 = jax.random.normal(ks[2], (E, D, F), dtype=jnp.float32) * (1.0 / math.sqrt(D))
        b1 = jnp.zeros((E, F), dtype=jnp.float32)
        w2 = jax.random.normal(ks[3], (E, F, D), dtype=jnp.float32) * (1.0 / math.sqrt(F))
        b2 = jnp.zeros((E, D), dtype=jnp.float32)
        return {'h': h, 'gate_w': gate_w, 'gate_b': gate_b, 'w1': w1, 'b1': b1, 'w2': w2, 'b2': b2}
    _L0_ffn_all = _L0_ffn_setup()
    _L0_ffn_in = {k: v for k, v in _L0_ffn_all.items() if k in ('gate_w', 'gate_b', 'w1', 'b1', 'w2', 'b2')}
    del _L0_ffn_all
    return {'x': x, 'L0_tok_conv1_w': _L0_tok_in['conv1_w'], 'L0_tok_conv1_b': _L0_tok_in['conv1_b'], 'L0_tok_bn_gamma': _L0_tok_in['bn_gamma'], 'L0_tok_bn_beta': _L0_tok_in['bn_beta'], 'L0_tok_bn_mean': _L0_tok_in['bn_mean'], 'L0_tok_bn_var': _L0_tok_in['bn_var'], 'L0_tok_conv2_w': _L0_tok_in['conv2_w'], 'L0_tok_conv2_b': _L0_tok_in['conv2_b'], 'L0_attn_Wq': _L0_attn_in['Wq'], 'L0_attn_bq': _L0_attn_in['bq'], 'L0_attn_Wk': _L0_attn_in['Wk'], 'L0_attn_bk': _L0_attn_in['bk'], 'L0_attn_Wv': _L0_attn_in['Wv'], 'L0_attn_bv': _L0_attn_in['bv'], 'L0_attn_Wo': _L0_attn_in['Wo'], 'L0_attn_bo': _L0_attn_in['bo'], 'L0_ffn_gate_w': _L0_ffn_in['gate_w'], 'L0_ffn_gate_b': _L0_ffn_in['gate_b'], 'L0_ffn_w1': _L0_ffn_in['w1'], 'L0_ffn_b1': _L0_ffn_in['b1'], 'L0_ffn_w2': _L0_ffn_in['w2'], 'L0_ffn_b2': _L0_ffn_in['b2']}

def reference(x, L0_tok_conv1_w, L0_tok_conv1_b, L0_tok_bn_gamma, L0_tok_bn_beta, L0_tok_bn_mean, L0_tok_bn_var, L0_tok_conv2_w, L0_tok_conv2_b, L0_attn_Wq, L0_attn_bq, L0_attn_Wk, L0_attn_bk, L0_attn_Wv, L0_attn_bv, L0_attn_Wo, L0_attn_bo, L0_ffn_gate_w, L0_ffn_gate_b, L0_ffn_w1, L0_ffn_b1, L0_ffn_w2, L0_ffn_b2):
    import jax
    import jax.numpy as jnp

    def _L0_tok_ref(x, conv1_w, conv1_b, bn_gamma, bn_beta, bn_mean, bn_var, conv2_w, conv2_b):
        import jax, jax.numpy as jnp
        import numpy as np
        K = 3
        PAD = (K - 1) // 2
        BN_EPS = 1e-05

        def _unfold(x):
            b, c, h, w = x.shape
            xp = jnp.pad(x, ((0, 0), (0, 0), (PAD, PAD), (PAD, PAD)))
            shifts = [xp[:, :, i:i + h, j:j + w] for i in range(K) for j in range(K)]
            return jnp.stack(shifts, axis=2)
        b, c, h, w = x.shape
        y = jnp.einsum('oc,bchw->bohw', conv1_w, x) + conv1_b[None, :, None, None]
        y = (y - bn_mean[None, :, None, None]) * (bn_gamma[None, :, None, None] * jax.lax.rsqrt(bn_var + BN_EPS)[None, :, None, None]) + bn_beta[None, :, None, None]
        y = jax.nn.relu(y)
        wdyn = jnp.einsum('ok,bkhw->bohw', conv2_w, y) + conv2_b[None, :, None, None]
        patches = _unfold(x)
        out = jnp.einsum('bckhw,bkhw->bchw', patches, wdyn)
        return out.reshape(b, h * w, c)

    def _L0_attn_ref(src, Wq, bq, Wk, bk, Wv, bv, Wo, bo):
        import jax, jax.numpy as jnp
        import numpy as np
        import math
        B, S, D = (4, 1024, 64)
        q = src @ Wq.T + bq
        k = src @ Wk.T + bk
        v = src @ Wv.T + bv
        row_mask = (q[:, :, 0] != 0) & (k[:, :, 0] != 0)
        mask = row_mask[:, :, None]
        scale = 1.0 / math.sqrt(D)
        scores = jnp.einsum('bid,bjd->bij', q, k) * scale
        scores = jnp.where(mask, scores, jnp.float32(-1000000000.0))
        prob = jax.nn.softmax(scores, axis=-1)
        prob = jnp.where(mask, prob, 0.0)
        out = jnp.einsum('bij,bjd->bid', prob, v)
        return out @ Wo.T + bo

    def _L0_ffn_ref(h, gate_w, gate_b, w1, b1, w2, b2):
        import math
        import jax, jax.numpy as jnp
        import numpy as np
        CAPACITY_FACTOR = 1.25
        B, L, D = h.shape
        E = gate_w.shape[1]
        T = B * L
        C = max(1, math.ceil(CAPACITY_FACTOR * T / E))
        x = h.reshape(T, D)
        logits = x @ gate_w + gate_b
        probs = jax.nn.softmax(logits, axis=-1)
        idx = jnp.argmax(probs, axis=-1)
        prb = jnp.take_along_axis(probs, idx[:, None], axis=1)[:, 0]
        one_hot = jax.nn.one_hot(idx, E, dtype=jnp.float32)
        pos = (jnp.cumsum(one_hot, axis=0) * one_hot).sum(-1).astype(jnp.int32) - 1
        kept = pos < C
        pos_safe = jnp.where(kept, pos, C)
        buf = jnp.zeros((E, C, D), dtype=h.dtype).at[idx, pos_safe].set(x, mode='drop')
        hmid = jax.nn.relu(jnp.einsum('ecd,edf->ecf', buf, w1) + b1[:, None, :])
        ybuf = jnp.einsum('ecf,efd->ecd', hmid, w2) + b2[:, None, :]
        pos_g = jnp.minimum(pos, C - 1)
        y_tok = ybuf[idx, pos_g] * (prb * kept)[:, None]
        y = y_tok.reshape(B, L, D)
        y = jnp.nan_to_num(y, nan=0.0, posinf=10000.0, neginf=-10000.0)
        return y
    h = _L0_tok_ref(x, L0_tok_conv1_w, L0_tok_conv1_b, L0_tok_bn_gamma, L0_tok_bn_beta, L0_tok_bn_mean, L0_tok_bn_var, L0_tok_conv2_w, L0_tok_conv2_b)
    h = h + _L0_attn_ref(_layernorm(h, axis=-1), L0_attn_Wq, L0_attn_bq, L0_attn_Wk, L0_attn_bk, L0_attn_Wv, L0_attn_bv, L0_attn_Wo, L0_attn_bo)
    h = h + _L0_ffn_ref(_layernorm(h, axis=-1), L0_ffn_gate_w, L0_ffn_gate_b, L0_ffn_w1, L0_ffn_b1, L0_ffn_w2, L0_ffn_b2)
    return h

_drawn_inputs = setup_inputs


def setup_inputs(seed=0):
    import zlib

    import numpy as np

    out = dict(_drawn_inputs(seed))
    spreads = {'L0_tok_conv1_b': (0.0, 0.1),
     'L0_tok_bn_gamma': (1.0, 0.2),
     'L0_tok_bn_beta': (0.0, 0.1),
     'L0_tok_bn_mean': (0.0, 0.1),
     'L0_tok_bn_var': (1.0, 0.2),
     'L0_tok_conv2_b': (0.0, 0.1),
     'L0_ffn_gate_b': (0.0, 0.1),
     'L0_ffn_b1': (0.0, 0.8),
     'L0_ffn_b2': (0.0, 0.8)}
    factors = {'L0_attn_bq': 5.809, 'L0_attn_bk': 8.0}
    for name, (base, spread) in spreads.items():
        noise = np.random.default_rng([zlib.crc32(name.encode()), seed]).standard_normal(out[name].shape)
        drawn = base * np.exp(spread * noise) if base else spread * noise
        out[name] = jnp.asarray(drawn.astype(out[name].dtype))
    for name, factor in factors.items():
        out[name] = (out[name] * factor).astype(out[name].dtype)
    return out
```

```python
from contextlib import ExitStack

import numpy as np
import concourse.bass as bass
from concourse import mybir

F32 = mybir.dt.float32
F32R = mybir.dt.float32r
F16 = mybir.dt.float16
I32 = mybir.dt.int32
ALU = mybir.AluOpType
ACT = mybir.ActivationFunctionType
AX = mybir.AxisListType

P = 128
LN_EPS = 1e-5
BN_EPS = 1e-5


class Order:

    def __init__(self, eng, sem, base):
        self.eng, self.sem, self.base, self.n = eng, sem, base, 0

    def did(self, ins):
        ins.then_inc(self.sem, 1)
        self.n += 1
        return self.n

    def need(self, n):
        self.eng.wait_ge(self.sem, self.base + n)

    def then(self, ins):
        self.need(self.did(ins))


def tower(nc, x, conv1_w, conv1_b, bn_gamma, bn_beta, bn_mean, bn_var, conv2_w, conv2_b,
          Wq, bq, Wk, bk, Wv, bv, Wo, bo, gate_w, gate_b, w1, b1, w2, b2, out, slots_x, slots_y):
    B, C, HH, WW = x.shape
    CR = conv1_w.shape[0]
    TAPS = conv2_w.shape[0]
    D = WW
    S = C * HH
    N = S // P
    RH = HH // 2
    E = gate_w.shape[1]
    F = w1.shape[2]
    CAP = -(-5 * B * S // (4 * E))
    GQ = 512
    G = S // GQ
    QT = GQ // P
    KC = S // 512
    STEPS = N // 2
    SCALE = float(D) ** -0.5
    LIFT = 8.0 * float(np.log(2.0)) / SCALE
    assert (B, C, HH, WW, CR, TAPS, E, F) == (4, 64, 64, 64, 16, 9, 8, 256)
    HALF = RH * WW
    PCH = HALF // 512
    FC = F // P
    CH = CAP // 512
    assert CH * 512 == CAP
    CENTER_FIRST = [4, 0, 1, 2, 3, 5, 6, 7, 8]
    LAG = 3
    RP = 4
    R32 = 3

    with ExitStack() as ctx:
        ctx.enter_context(nc.allow_non_contiguous_dma(reason="small weights, loaded once"))
        def sb(name, shape, dt=F32):
            return ctx.enter_context(nc.sbuf_tensor(name, shape, dt))

        def psum(name, shape):
            return ctx.enter_context(nc.psum_tensor(name, shape, F32))

        def sem(name):
            return ctx.enter_context(nc.semaphore(name))

        ps_s = psum("ps_s", [P, 4, 512])
        ps_a = psum("ps_a", [P, 2, 512])
        ps_o = psum("ps_o", [P, 512])
        ps_m = psum("ps_m", [P, 512])

        ident = sb("ident", [P, P])
        before = sb("before", [P, P])
        ones = sb("ones", [P, P])
        w_nat = sb("w_nat", [D, 4, D])
        wqT = sb("wqT", [D, 2, D])
        wkT = sb("wkT", [D, 2, D])
        woT = sb("woT", [D, D])
        wvx = sb("wvx", [D, P])
        wg = sb("wg", [P, D + 2])
        bq2 = sb("bq2", [P, 1])
        bk2 = sb("bk2", [P, 1])
        bo_all = sb("bo_all", [P, D])
        lift = sb("lift", [P, 1])
        w1bd = sb("w1bd", [P, 48])
        bn_raw = sb("bn_raw", [48, 5])
        bn_t = sb("bn_t", [48, 4])
        bn_scale = sb("bn_scale", [48, 1])
        bn_bias = sb("bn_bias", [48, 1])
        cw2 = sb("cw2", [65, TAPS])
        tapw = sb("tapw", [65, TAPS, C, 2])
        gw = sb("gw", [D, E])
        gb_all = sb("gb_all", [P, E])
        e_down = sb("e_down", [P, E])
        e_base = sb("e_base", [P, E])
        b1c = sb("b1c", [P, E, FC])
        b2c = sb("b2c", [D, E])

        xh = sb("xh", [P, RH + 2, WW])
        xc = sb("xc", [P, HALF])
        y = sb("y", [65, HALF])
        tmp = sb("tmp", [P, 2, 8, WW])
        h = sb("h", [P, B * N, D])
        xcen = sb("xcen", [P, N, D])
        xn = sb("xn", [P, N, D])
        zeros = xcen[:].rearrange("p n d -> p (n d)")
        ln_s = sb("ln_s", [P, 6, N])
        xs = sb("xs", [P, N, P], F16)
        xT = sb("xT", [D, S])
        kh = sb("kh", [P, S], F32R)
        kl = sb("kl", [65, S], F32R)
        q1 = sb("q1", [P, 2, GQ], F32R)
        q2 = sb("q2", [65, 2, GQ], F32R)
        live_q = sb("live_q", [65, 2, GQ])
        live = sb("live", [65, 2, GQ])
        mx = sb("mx", [P, QT, KC])
        rowmax = sb("rowmax", [P, QT])
        p32 = sb("p32", [P, R32, 1024])
        ph = sb("ph", [P, RP, 1024], F16)
        pl = sb("pl", [P, RP, 1024], F16)
        oT = sb("oT", [P, GQ])
        post = sb("post", [P, 2, QT])
        att = sb("att", [P, QT, D])

        lg = sb("lg", [P, N, E])
        rt = sb("rt", [P, 6, N])
        oneh = sb("oneh", [P, N, E])
        cum = sb("cum", [P, 2, N, E])
        carry = sb("carry", [P, E])
        cbase = sb("cbase", [P, E])
        weight = sb("weight", [P, B * N])
        put_at = sb("put_at", [P, N], I32)
        get_at = sb("get_at", [P, B * N], I32)

        w1s = sb("w1s", [D, 2, F])
        w2s = sb("w2s", [P, 2, FC, D])
        xm = sb("xm", [P, 2, 4, D])
        ym = sb("ym", [P, 2, 4, D])
        xmT = xT[:, 0:512]
        yT = xT[:, 512:1024]
        hid = p32[:, 2, :].rearrange("p (f s) -> p f s", f=FC)
        bad = xc[:].rearrange("p (n d) -> p n d", d=D).bitcast(I32)

        consts_in = sem("consts_in")
        zero_out = sem("zero_out")
        made = sem("made")
        cleared = sem("cleared")
        s_dset = sem("s_dset")
        s_pset = sem("s_pset")
        s_aset = sem("s_aset")
        x_in = sem("x_in")
        x_free = sem("x_free")
        conv1 = sem("conv1")
        y_ready = sem("y_ready")
        tap_full = sem("tap_full")
        tap_used = sem("tap_used")
        s_dve1 = sem("s_dve1")
        var_ready = sem("var_ready")
        sd_ready = sem("sd_ready")
        xn_ready = sem("xn_ready")
        xt_full = sem("xt_full")
        xt_ready = sem("xt_ready")
        k_full = sem("k_full")
        kh_ready = sem("kh_ready")
        kl_ready = sem("kl_ready")
        xs_ready = sem("xs_ready")
        q_full = sem("q_full")
        qh_ready = sem("qh_ready")
        q_ready = sem("q_ready")
        a_full = sem("a_full")
        a_used = sem("a_used")
        max_ready = sem("max_ready")
        mrow_full = sem("mrow_full")
        mrow_ready = sem("mrow_ready")
        s_full = sem("s_full")
        ph_ready = sem("ph_ready")
        pl_ready = sem("pl_ready")
        av_done = sem("av_done")
        oT_ready = sem("oT_ready")
        live_in = sem("live_in")
        post_full = sem("post_full")
        s_dve2 = sem("s_dve2")
        h_ready = sem("h_ready")
        lg_full = sem("lg_full")
        lg_centred = sem("lg_centred")
        lg_exp = sem("lg_exp")
        s_dve3 = sem("s_dve3")
        cp_ready = sem("cp_ready")
        cb_full = sem("cb_full")
        put_ready = sem("put_ready")
        put_done = sem("put_done")
        xn_free = sem("xn_free")
        w_in = [sem("w_in0"), sem("w_in1")]
        xm_in = [sem("xm_in0"), sem("xm_in1")]
        xmT_full = sem("xmT_full")
        xmT_ready = sem("xmT_ready")
        hid_full = sem("hid_full")
        hid_a = sem("hid_a")
        hid_b = sem("hid_b")
        yT_full = sem("yT_full")
        yT_ready = sem("yT_ready")
        ym_full = sem("ym_full")
        ym_ready = sem("ym_ready")
        y_out = [sem("y_out0"), sem("y_out1")]
        got = sem("got")
        s_dve4 = sem("s_dve4")
        out_ready = sem("out_ready")
        stored = sem("stored")
        waits = {e.engine: sem(f"waits_{n}") for n, e in (("pe", nc.tensor), ("act", nc.scalar),
                                                          ("dve", nc.vector), ("pool", nc.gpsimd))}

        def wait_apart(eng, semaphore, value):
            eng.wait_ge(semaphore, value)
            eng.sem_inc(waits[eng.engine], 1)

        def images(eng, prepare, group, finish):
            with eng.Fori(0, B) as b:
                prepare(b)
                with eng.Fori(0, G // 2 - 1) as pair:
                    group(b, pair * 2, 0, False)
                    group(b, pair * 2 + 1, 1, False)
                group(b, G - 2, 0, False)
                group(b, G - 1, 1, True)
                finish(b)

        def has_query_product(g):
            return not (isinstance(g, int) and g + 2 >= G)

        def step0(b, g):
            return (b * G + g) * STEPS

        N_CONST = 29
        ND1 = PCH * (TAPS - 1) + 7
        ND2 = 4
        ND3 = 36

        block = ctx.enter_context(nc.Block())

        @block.sync
        def _(sp):
            for i, w in enumerate((Wq, Wk, Wv, Wo)):
                sp.dma_start(w_nat[:, i, :], w).then_inc(consts_in, 16)
            for dst, v in ((bq2, bq), (bk2, bk)):
                for half in range(2):
                    sp.dma_start(dst[D * half:D * (half + 1), :], v.rearrange("(a b) -> a b", b=1)).then_inc(consts_in, 16)
            sp.wait_ge(made, 4)
            for half in range(2):
                sp.dma_start(w1bd[C * half:C * (half + 1), 32 * half:32 * half + CR],
                             conv1_w.rearrange("o c -> c o")).then_inc(consts_in, 16)
                for i, v in enumerate((conv1_b, bn_gamma, bn_beta, bn_mean, bn_var)):
                    sp.dma_start(bn_raw[32 * half:32 * half + CR, i:i + 1],
                                 v.rearrange("(a b) -> a b", b=1)).then_inc(consts_in, 16)
                sp.dma_start(cw2[32 * half:32 * half + CR, :], conv2_w.rearrange("k o -> o k")).then_inc(consts_in, 16)
            sp.dma_start(cw2[64:65, :], conv2_b.rearrange("(b a) -> b a", b=1)).then_inc(consts_in, 16)
            sp.dma_start(wvx[:, 63:64], bv.rearrange("(a b) -> a b", b=1)).then_inc(consts_in, 16)
            sp.dma_start(bo_all[:], bo.partition_broadcast(P)).then_inc(consts_in, 16)
            sp.dma_start(gb_all[:], gate_b.partition_broadcast(P)).then_inc(consts_in, 16)
            sp.dma_start(gw[:], gate_w).then_inc(consts_in, 16)
            sp.dma_start(b1c[:], b1.rearrange("e (f p) -> p e f", p=P)).then_inc(consts_in, 16)
            sp.dma_start(b2c[:], b2.rearrange("e d -> d e")).then_inc(consts_in, 16)

            sp.wait_ge(cleared, 1)
            with sp.Fori(0, B) as b:
                sp.wait_ge(x_free, b + 1)
                for half in range(2):
                    lo = 0 if half == 0 else RH - 1
                    sp.dma_start(
                        xh[half:P:2, 1 - half:RH + 2 - half, :],
                        x[bass.ds(b, 1), :, lo:lo + RH + 1, :].rearrange("a c r w -> (a c) r w")).then_inc(x_in, 16)
                    sp.dma_start(
                        xc[C * half:C * (half + 1), :],
                        x[bass.ds(b, 1), :, RH * half:RH * (half + 1), :].rearrange("a c r w -> (a c) (r w)"),
                    ).then_inc(x_in, 16)

            with sp.Fori(0, E // 2) as pair:
                for par in range(2):
                    sp.wait_ge(ym_full, pair * 2 * CH + 1)
                    e = pair * 2 + par
                    sp.dma_start(w1s[:, par, :], w1[bass.ds(e, 1)].rearrange("a d f -> (a d) f")).then_inc(w_in[par], 16)
                    sp.dma_start(w2s[:, par, :, :], w2[bass.ds(e, 1)].rearrange("a (f p) d -> p (a f) d", p=P)).then_inc(w_in[par], 16)
                    for a in range(CH):
                        c = par * CH + a
                        k = pair * (2 * CH) + c
                        if c < 2:
                            sp.wait_ge(put_done, 16 * N * B)
                        sp.wait_ge(xmT_full, k + (0 if c >= 1 else 1))
                        sp.dma_start(xm[:, c % 2, :, :],
                                     slots_x[bass.ds(k * 512, 512), :].rearrange("(p a) d -> p a d", p=P),
                                     ).then_inc(xm_in[c % 2], 16)
                        if c >= 1:
                            sp.wait_ge(ym_ready, k)
                            sp.dma_start(slots_y[bass.ds((k - 1) * 512, 512), :].rearrange("(p a) d -> p a d", p=P),
                                         ym[:, (c - 1) % 2, :, :]).then_inc(y_out[(c - 1) % 2], 16)
                k = pair * (2 * CH) + 2 * CH - 1
                sp.wait_ge(ym_ready, k + 1)
                sp.dma_start(slots_y[bass.ds(k * 512, 512), :].rearrange("(p a) d -> p a d", p=P),
                             ym[:, 1, :, :]).then_inc(y_out[1], 16)

            for b in range(B):
                sp.wait_ge(out_ready, b + 1)
                sp.dma_start(out[b].rearrange("(p n) d -> p n d", p=P), h[:, b * N:(b + 1) * N, :]).then_inc(stored, 16)
            sp.wait_ge(stored, 16 * B)
            sp.wait_ge(zero_out, 32 * B)

        @block.gpsimd
        def _(pool):
            pool.sem_inc(xn_free, 1)
            pool.memset(bn_raw[:], 0.0).then_inc(made, 1)
            pool.memset(w1bd[:], 0.0).then_inc(made, 1)
            pool.memset(wvx[:], 0.0).then_inc(made, 1)
            pool.memset(cw2[:], 0.0).then_inc(made, 1)
            pool.memset(ones[:], 1.0).then_inc(made, 1)
            pool.memset(zeros, 0.0).then_inc(made, 1)
            pool.wait_ge(made, 6)
            pool.affine_select(out=ident[:], in_=ones[:], compare_op=ALU.is_equal, fill=0.0, base=0,
                               pattern=[[1, P]], channel_multiplier=-1).then_inc(made, 1)
            pool.affine_select(out=before[:], in_=ones[:], compare_op=ALU.is_gt, fill=0.0, base=0,
                               pattern=[[1, P]], channel_multiplier=-1).then_inc(made, 1)
            pool.iota(e_down[:], pattern=[[-1, E]], base=E, channel_multiplier=0,
                      allow_small_or_imprecise_dtypes=True).then_inc(made, 1)
            pool.iota(e_base[:], pattern=[[CAP, E]], base=0, channel_multiplier=0,
                      allow_small_or_imprecise_dtypes=True).then_inc(made, 1)

            def prepare(b):
                pass

            def group(b, g, par, last):
                t0 = step0(b, g)
                for j in range(STEPS):
                    pool.wait_ge(ph_ready, t0 + j + 1)
                    pool.tensor_tensor(out=pl[:, j % RP, :], in0=p32[:, j % R32, :], in1=ph[:, j % RP, :],
                                       op=ALU.subtract).then_inc(pl_ready, 1)

            def finish(b):
                pool.wait_ge(zero_out, 32 * B)
                wait_apart(pool, put_ready, b + 1)
                for n in range(N):
                    pool.indirect_dma_start(slots_x, bass.IndirectOffsetOnAxis(ap=put_at[:, n:n + 1], axis=0),
                                            xn[:, n, :], None, bounds_check=E * CAP - 1,
                                            oob_is_err=False).then_inc(put_done, 16)
                pool.wait_ge(put_done, (b + 1) * (16 * N))
                pool.sem_inc(xn_free, 1)

            images(pool, prepare, group, finish)

            pool.wait_ge(y_out[0], 16 * (E * CH // 2 + 1))
            pool.wait_ge(y_out[1], 16 * (E * CH // 2 + 1))
            for b in range(B):
                yg = (xn, xcen)[b % 2]
                if b >= 2:
                    pool.wait_ge(out_ready, b - 1)
                for n in range(N):
                    pool.indirect_dma_start(yg[:, n, :], None, slots_y,
                                            bass.IndirectOffsetOnAxis(ap=get_at[:, b * N + n:b * N + n + 1], axis=0),
                                            ).then_inc(got, 16)
                pool.wait_ge(got, 16 * N * (b + 1))

        @block.tensor
        def _(pe):
            pe.wait_ge(made, 8)
            pe.wait_ge(consts_in, 16 * N_CONST)
            for i, w in enumerate((0, 1, 3)):
                last = pe.transpose(ps_m[0:D, D * i:D * (i + 1)], w_nat[:, w, :], ident[0:D, 0:D])
            last.then_inc(s_pset, 1)
            pe.wait_ge(s_dset, 1)
            pe.matmul(ps_m[:, 256:256 + D], wvx[:], woT[:], start=True, stop=True).then_inc(s_pset, 1)

            def q_product(b, g):
                pe.matmul(ps_m[:], wqT[:], xT[:, bass.ds(g * GQ, GQ)], start=True, stop=True).then_inc(q_full, 1)

            def a_product(b, g, par, a):
                if a == 0:
                    pe.wait_ge(q_ready, b * G + g + 1)
                if a >= 2:
                    pe.wait_ge(a_used, (b * G + g) * (QT * KC) + a - 1)
                qt, kc = a // KC, a % KC
                pe.matmul(ps_a[:, a % 2, :], q1[:, par, qt * P:(qt + 1) * P], kh[:, kc * 512:(kc + 1) * 512],
                          start=True, stop=True).then_inc(a_full, 1)

            def max_rows(b, g):
                pe.wait_ge(max_ready, b * G + g + 1)
                for qt in range(QT):
                    mm = pe.matmul(ps_m[64:65, qt * P:(qt + 1) * P], rowmax[:, qt:qt + 1], ident[:],
                                   start=True, stop=True)
                mm.then_inc(mrow_full, 1)

            def prepare(b):
                pe.wait_ge(x_in, 64 * (b + 1))
                for i in range(PCH):
                    pe.matmul(ps_s[0:48, i, :], w1bd[:], xc[:, i * 512:(i + 1) * 512],
                              start=True, stop=True).then_inc(conv1, 1)
                for i in range(PCH):
                    pe.wait_ge(y_ready, PCH * b + i + 1)
                    for kk, k in enumerate(CENTER_FIRST):
                        t = i * TAPS + kk
                        if t >= 2:
                            pe.wait_ge(tap_used, PCH * TAPS * b + t - 1)
                        pe.matmul(ps_a[:, t % 2, :], tapw[:, k, :, :], y[:, i * 512:(i + 1) * 512],
                                  start=True, stop=True).then_inc(tap_full, 1)
                transposed(b, 0)
                for c in range(KC):
                    if c >= 2:
                        pe.wait_ge(kl_ready, KC * b + c - 1)
                    pe.matmul(ps_a[:, c % 2, :], wkT[:], xT[:, c * 512:(c + 1) * 512],
                              start=True, stop=True).then_inc(k_full, 1)
                q_product(b, 0)
                pe.wait_ge(kl_ready, KC * (b + 1))
                for a in range(QT * KC):
                    a_product(b, 0, 0, a)
                max_rows(b, 0)
                pe.wait_ge(mrow_ready, b * G + 1)
                q_product(b, 1)

            def transposed(b, which):
                wait_apart(pe, xn_ready, 2 * b + which + 1)
                for c in range(KC):
                    if c >= 4:
                        wait_apart(pe, xt_ready, (2 * b + which) * KC + c - 3)
                    for i in range(4):
                        mm = pe.transpose(ps_s[0:D, c % 4, i * P:(i + 1) * P], xn[:, 4 * c + i, :], ident[:])
                    mm.then_inc(xt_full, 1)
                pe.wait_ge(xt_ready, (2 * b + which + 1) * KC)

            def group(b, g, par, last):
                t0 = step0(b, g)

                def scores(j):
                    if j == 0:
                        pe.wait_ge(mrow_ready, b * G + g + 1)
                    if j >= 2:
                        pe.wait_ge(ph_ready, t0 + j - 1)
                    for i in range(2):
                        n = 2 * j + i
                        dst = ps_s[:, 2 * (j % 2) + i, :]
                        pe.matmul(dst, kh[:, n * P:(n + 1) * P], q1[:, par, :], start=True, stop=False)
                        mm = pe.matmul(dst, kl[:, n * P:(n + 1) * P], q2[:, par, :], start=False, stop=True)
                    mm.then_inc(s_full, 1)

                def weigh(j):
                    pe.wait_ge(ph_ready, t0 + j + 1)
                    for i in range(2):
                        pe.matmul(ps_o[:], xs[:, 2 * j + i, :], ph[:, j % RP, i * 512:(i + 1) * 512],
                                  start=(j == 0 and i == 0), stop=False)
                    pe.wait_ge(pl_ready, t0 + j + 1)
                    for i in range(2):
                        mm = pe.matmul(ps_o[:], xs[:, 2 * j + i, :], pl[:, j % RP, i * 512:(i + 1) * 512],
                                       start=False, stop=(j == STEPS - 1 and i == 1))
                    mm.then_inc(av_done, 1)

                a = 0
                for j in range(STEPS + LAG):
                    if j < STEPS:
                        scores(j)
                    if not last:
                        for _ in range(3):
                            if j >= 1 and a < QT * KC:
                                a_product(b, g + 1, 1 - par, a)
                                a += 1
                        if j == 13:
                            max_rows(b, g + 1)
                    if j == STEPS and not last:
                        pe.wait_ge(mrow_ready, b * G + g + 2)
                        if has_query_product(g):
                            q_product(b, g + 2)
                    if j >= LAG:
                        weigh(j - LAG)
                pe.wait_ge(live_in, b * G + g + 1)
                if has_query_product(g):
                    pe.wait_ge(q_ready, b * G + g + 3)
                for qt in range(QT):
                    mm = pe.matmul(ps_m[:, qt * (D + 2):(qt + 1) * (D + 2)], oT[:, qt * P:(qt + 1) * P], wg[:],
                                   start=True, stop=True)
                mm.then_inc(post_full, 1)
                pe.wait_ge(h_ready, b * G + g + 1)

            def finish(b):
                transposed(b, 1)
                for n in range(N):
                    mm = pe.matmul(ps_m[:, n * E:(n + 1) * E], xT[:, n * P:(n + 1) * P], gw[:],
                                   start=True, stop=True)
                mm.then_inc(lg_full, 1)
                pe.wait_ge(cp_ready, b + 1)
                pe.matmul(ps_m[:, N * E:(N + 1) * E], before[:], cum[:, 1, N - 1, :], start=True, stop=False)
                pe.matmul(ps_m[:, N * E:(N + 1) * E], ones[:], carry[:], start=False, stop=True).then_inc(cb_full, 1)

            images(pe, prepare, group, finish)

            pe.sem_inc(ym_full, 1)
            pe.sem_inc(xmT_full, 1)
            with pe.Fori(0, E // 2) as pair:
                for par in range(2):
                    e = pair * 2 + par
                    pe.wait_ge(w_in[par], (pair + 1) * 32)
                    for a in range(CH):
                        c = par * CH + a
                        k = pair * (2 * CH) + c
                        wait_apart(pe, xm_in[c % 2], (pair * CH + c // 2 + 1) * 16)
                        for i in range(4):
                            mm = pe.transpose(ps_s[0:D, 0, i * P:(i + 1) * P], xm[:, c % 2, i, :], ident[:])
                        mm.then_inc(xmT_full, 1)
                        pe.wait_ge(xmT_ready, k + 1)
                        for f in range(FC):
                            pe.matmul(ps_s[:, 1 + f, :], w1s[:, par, f * P:(f + 1) * P], xmT,
                                      start=True, stop=True).then_inc(hid_full, 1)
                        pe.wait_ge(hid_a, k + 1)
                        pe.matmul(ps_s[0:D, 3, :], w2s[:, par, 0, :], hid[:, 0, :], start=True, stop=False)
                        pe.wait_ge(hid_b, k + 1)
                        pe.matmul(ps_s[0:D, 3, :], w2s[:, par, 1, :], hid[:, 1, :], start=False,
                                  stop=True).then_inc(yT_full, 1)
                        wait_apart(pe, yT_ready, k + 1)
                        for i in range(4):
                            mm = pe.transpose(ps_m[:, i * D:(i + 1) * D], yT[:, i * P:(i + 1) * P], ident[0:D, 0:D])
                        mm.then_inc(ym_full, 1)

        @block.scalar
        def _(act):
            rows = E * CAP // B
            act.wait_ge(made, 6)
            for b in range(B):
                part = slots_x[b * rows:(b + 1) * rows, :].rearrange("(p a) d -> p (a d)", p=P)
                act.dma_start(part[:, 0:2048], zeros).then_inc(zero_out, 16)
                act.dma_start(part[:, 2048:rows * D // P], zeros[:, 0:rows * D // P - 2048]).then_inc(zero_out, 16)
            act.wait_ge(s_dset, 2)
            act.activation(bn_t[:, 1:2], bn_t[:, 0:1], ACT.Sqrt).then_inc(s_aset, 1)

            def root(b, which):
                act.wait_ge(var_ready, 2 * b + which + 1)
                act.activation(ln_s[:, 4, :], ln_s[:, 3, :], ACT.Sqrt).then_inc(sd_ready, 1)

            def take_xT(b, which):
                for c in range(KC):
                    act.wait_ge(xt_full, (2 * b + which) * KC + c + 1)
                    act.activation(xT[:, c * 512:(c + 1) * 512], ps_s[0:D, c % 4, :], ACT.Copy).then_inc(xt_ready, 1)

            def take_q(b, g, par):
                act.wait_ge(q_full, b * G + g + 1)
                act.activation(q2[0:D, par, :], ps_m[0:D, :], ACT.Identity, bias=bq2[0:D, :])
                act.activation(q1[:, par, :], ps_m[:], ACT.Identity, bias=bq2[:]).then_inc(qh_ready, 1)

            def take_max(b, g, par):
                act.wait_ge(mrow_full, b * G + g + 1)
                act.activation(q2[D:D + 1, par, :], ps_m[D:D + 1, :], ACT.Identity, bias=lift[D:D + 1, :],
                               scale=-1.0).then_inc(mrow_ready, 1)

            def prepare(b):
                for i in range(PCH):
                    act.wait_ge(conv1, PCH * b + i + 1)
                    if i == 0:
                        act.wait_ge(s_dset, 5)
                    act.activation(y[0:48, i * 512:(i + 1) * 512], ps_s[0:48, i, :], ACT.Relu,
                                   bias=bn_bias[:], scale=bn_scale[:]).then_inc(y_ready, 1)
                root(b, 0)
                take_xT(b, 0)
                for c in range(KC):
                    act.wait_ge(k_full, KC * b + c + 1)
                    act.activation(kh[:, c * 512:(c + 1) * 512], ps_a[:, c % 2, :], ACT.Identity,
                                   bias=bk2[:]).then_inc(kh_ready, 1)
                take_q(b, 0, 0)
                take_max(b, 0, 0)
                take_q(b, 1, 1)

            def group(b, g, par, last):
                t0 = step0(b, g)
                for j in range(STEPS):
                    act.wait_ge(s_full, t0 + j + 1)
                    if j >= R32:
                        act.wait_ge(pl_ready, t0 + j - R32 + 1)
                    act.activation(p32[:, j % R32, :], ps_s[:, 2 * (j % 2):2 * (j % 2) + 2, :], ACT.Exp, scale=SCALE)
                    if j >= RP:
                        act.wait_ge(av_done, t0 + j - RP + 1)
                    act.activation(ph[:, j % RP, :], ps_s[:, 2 * (j % 2):2 * (j % 2) + 2, :], ACT.Exp,
                                   scale=SCALE).then_inc(ph_ready, 1)
                    if j == 13 and not last:
                        take_max(b, g + 1, 1 - par)
                if has_query_product(g):
                    take_q(b, g + 2, par)
                act.wait_ge(av_done, t0 + STEPS)
                act.activation(oT[:], ps_o[:], ACT.Copy).then_inc(oT_ready, 1)

            def finish(b):
                root(b, 1)
                take_xT(b, 1)
                act.wait_ge(lg_centred, b + 1)
                act.activation(cum[:, 0, :, :], lg[:], ACT.Exp).then_inc(lg_exp, 1)

            images(act, prepare, group, finish)

            act.sem_inc(y_out[0], 16)
            act.sem_inc(y_out[1], 16)
            with act.Fori(0, E // 2) as pair:
                for par in range(2):
                    for a in range(CH):
                        c = par * CH + a
                        k = pair * (2 * CH) + c
                        act.wait_ge(xmT_full, k + 2)
                        act.activation(xmT, ps_s[0:D, 0, :], ACT.Copy).then_inc(xmT_ready, 1)
                        wait_apart(act, hid_full, (k + 1) * 2 - 1)
                        act.activation(hid[:, 0, :], ps_s[:, 1, :], ACT.Relu,
                                       bias=b1c[:, bass.ds(pair * 2 + par, 1), 0:1].rearrange("p a b -> p (a b)")
                                       ).then_inc(hid_a, 1)
                        act.wait_ge(ym_full, k + 2)
                        act.wait_ge(y_out[c % 2], (pair * CH + c // 2 + 1) * 16)
                        act.activation(ym[:, c % 2, :, :], ps_m[:, 0:4 * D], ACT.Copy).then_inc(ym_ready, 1)

        @block.vector
        def _(dve):
            dve.memset(lift[:], LIFT)
            dve.memset(carry[:], 0.0)
            dve.memset(xh[:, 0:1, :], 0.0)
            dve.memset(xh[:, RH + 1:RH + 2, :], 0.0)
            dve.memset(y[0:64, :], 0.0)
            dve.memset(y[64:65, :], 1.0)
            dve.memset(kl[64:65, :].bitcast(F32), 1.0)
            dve.memset(xs[:], 0.0)
            dve.memset(tapw[:], 0.0).then_inc(cleared, 1)
            dve.wait_ge(cleared, 1)
            dve.sem_inc(x_free, 1)

            setup = Order(dve, s_dset, 0)
            dve.wait_ge(consts_in, 16 * N_CONST)
            dve.wait_ge(made, 10)
            dve.wait_ge(s_pset, 1)
            dve.tensor_copy(wqT[:, 0, :], ps_m[0:D, 0:D])
            dve.tensor_copy(wqT[:, 1, :], ps_m[0:D, 0:D])
            dve.tensor_copy(wkT[:, 0, :], ps_m[0:D, D:2 * D])
            dve.tensor_copy(wkT[:, 1, :], ps_m[0:D, D:2 * D])
            dve.tensor_copy(wg[:, D:D + 2], ident[:, 63:65])
            dve.tensor_copy(woT[:], ps_m[0:D, 2 * D:3 * D])
            dve.tensor_scalar(wvx[:, 0:63], w_nat[:, 2, 0:63], w_nat[:, 2, 63:64], None, ALU.subtract)
            setup.did(dve.tensor_scalar(wvx[:, 65:128], w_nat[:, 2, 0:63], w_nat[:, 2, 63:64], None, ALU.subtract))
            dve.memset(xs[:, :, 63:64], 1.0)
            setup.did(dve.tensor_scalar(bn_t[:, 0:1], bn_raw[:, 4:5], BN_EPS, None, ALU.add))
            dve.tensor_tensor(bn_t[:, 3:4], bn_raw[:, 0:1], bn_raw[:, 3:4], ALU.subtract)
            dve.wait_ge(s_aset, 1)
            setup.then(dve.reciprocal(bn_t[:, 2:3], bn_t[:, 1:2]))
            setup.did(dve.tensor_tensor(bn_scale[:], bn_raw[:, 1:2], bn_t[:, 2:3], ALU.mult))
            for half in range(2):
                dve.tensor_copy(tapw[32 * half:32 * half + CR, :, :, half],
                                cw2[32 * half:32 * half + CR, :].unsqueeze(2).to_broadcast([CR, TAPS, C]))
            dve.tensor_copy(tapw[64:65, :, :, 0], cw2[64:65, :].unsqueeze(2).to_broadcast([1, TAPS, C]))
            dve.tensor_copy(tapw[64:65, :, :, 1], cw2[64:65, :].unsqueeze(2).to_broadcast([1, TAPS, C]))
            setup.need(4)
            dve.scalar_tensor_tensor(out=bn_bias[:], in0=bn_t[:, 3:4], scalar=bn_scale[:], in1=bn_raw[:, 2:3],
                                     op0=ALU.mult, op1=ALU.add).then_inc(s_dset, 1)
            dve.wait_ge(s_pset, 2)
            dve.tensor_copy(wg[:, 0:D], ps_m[:, 256:256 + D]).then_inc(s_dset, 1)

            def spread(v):
                return v.unsqueeze(2).to_broadcast([P, N, D])

            def layer_norm(order, src, b, which):
                order.then(dve.tensor_reduce(ln_s[:, 0, :], src, AX.X, ALU.add))
                order.then(dve.tensor_scalar(ln_s[:, 1, :], ln_s[:, 0, :], 1.0 / D, None, ALU.mult))
                order.then(dve.tensor_tensor(xcen[:], src, spread(ln_s[:, 1, :]), ALU.subtract))
                order.then(dve.tensor_tensor(xn[:], xcen[:], xcen[:], ALU.mult))
                order.then(dve.tensor_reduce(ln_s[:, 2, :], xn[:], AX.X, ALU.add))
                dve.tensor_scalar(ln_s[:, 3, :], ln_s[:, 2, :], 1.0 / D, LN_EPS, ALU.mult, ALU.add).then_inc(var_ready, 1)
                dve.wait_ge(sd_ready, 2 * b + which + 1)
                order.then(dve.reciprocal(ln_s[:, 5, :], ln_s[:, 4, :]))
                dve.tensor_tensor(xn[:], xcen[:], spread(ln_s[:, 5, :]), ALU.mult).then_inc(xn_ready, 1)

            def prepare(b):
                order = Order(dve, s_dve1, b * ND1)
                dve.wait_ge(x_in, 64 * (b + 1))
                for i in range(PCH):
                    mine = h[:, bass.ds(b * N + 8 * i, 8), :]
                    for kk, k in enumerate(CENTER_FIRST):
                        t = i * TAPS + kk
                        dr, dc = k // 3, k % 3 - 1
                        w0, w1_ = max(0, -dc), min(WW, WW - dc)
                        wd = ps_a[:, t % 2, :].rearrange("p (r w) -> p r w", w=WW)[:, :, w0:w1_]
                        src = xh[:, 8 * i + dr:8 * i + dr + 8, w0 + dc:w1_ + dc]
                        dve.wait_ge(tap_full, PCH * TAPS * b + t + 1)
                        if kk == 0:
                            dve.tensor_tensor(mine, wd, src, ALU.mult).then_inc(tap_used, 1)
                            continue
                        dve.tensor_tensor(tmp[:, kk % 2, :, w0:w1_], wd, src, ALU.mult).then_inc(tap_used, 1)
                        dve.wait_ge(tap_used, PCH * TAPS * b + t + 1)
                        order.then(dve.tensor_tensor(mine[:, :, w0:w1_], mine[:, :, w0:w1_],
                                                     tmp[:, kk % 2, :, w0:w1_], ALU.add))
                dve.sem_inc(x_free, 1)
                dve.wait_ge(zero_out, 32 * B)
                wait_apart(dve, xn_free, b + 1)
                layer_norm(order, h[:, bass.ds(b * N, N), :], b, 0)
                dve.wait_ge(xn_ready, 2 * b + 1)
                order.then(dve.tensor_copy(xs[:, :, 0:63], xn[:, :, 0:63]))
                dve.tensor_tensor(xs[:, :, 65:128], xn[:, :, 0:63], xs[:, :, 0:63], ALU.subtract).then_inc(xs_ready, 1)
                assert order.n == ND1, order.n
                for c in range(KC):
                    dve.wait_ge(kh_ready, KC * b + c + 1)
                    dve.scalar_tensor_tensor(out=kl[0:D, c * 512:(c + 1) * 512], in0=ps_a[0:D, c % 2, :],
                                             scalar=bk2[0:D, :], in1=kh[0:D, c * 512:(c + 1) * 512].bitcast(F32),
                                             op0=ALU.add, op1=ALU.subtract).then_inc(kl_ready, 1)
                low_q(b, 0, 0)
                new_live(b, 0, 0)
                for a in range(QT * KC):
                    reduce_a(b, 0, a)
                whole_max(b, 0)
                low_q(b, 1, 1)
                new_live(b, 1, 1)

            def reduce_a(b, g, a):
                dve.wait_ge(a_full, (b * G + g) * (QT * KC) + a + 1)
                dve.tensor_reduce(mx[:, a // KC, a % KC:a % KC + 1], ps_a[:, a % 2, :], AX.X, ALU.max).then_inc(a_used, 1)

            def whole_max(b, g):
                dve.wait_ge(a_used, (b * G + g + 1) * (QT * KC))
                dve.tensor_reduce(rowmax[:], mx[:], AX.X, ALU.max).then_inc(max_ready, 1)

            def group(b, g, par, last):
                order = Order(dve, s_dve2, (b * G + g) * ND2)
                if not last:
                    for a in range(QT * KC):
                        reduce_a(b, g + 1, a)
                    whole_max(b, g + 1)
                mine = h[:, bass.ds(b * N + g * QT, QT), :]
                more = has_query_product(g)
                if more:
                    low_q(b, g + 2, par)
                dve.wait_ge(oT_ready, b * G + g + 1)
                dve.tensor_copy(oT[D:D + 1, :], live[D:D + 1, par, :]).then_inc(live_in, 1)
                if more:
                    dve.wait_ge(live_in, b * G + g + 1)
                    new_live(b, g + 2, par)
                dve.wait_ge(post_full, b * G + g + 1)
                got_o = ps_m[:, 0:QT * (D + 2)].rearrange("p (q d) -> p q d", d=D + 2)
                order.then(dve.reciprocal(post[:, 0, :], got_o[:, :, D:D + 1].rearrange("p q a -> p (q a)")))
                order.then(dve.tensor_tensor(post[:, 1, :], post[:, 0, :],
                                             got_o[:, :, D + 1:D + 2].rearrange("p q a -> p (q a)"), ALU.mult))
                order.then(dve.tensor_tensor(att[:], got_o[:, :, 0:D],
                                             post[:, 1, :].unsqueeze(2).to_broadcast([P, QT, D]), ALU.mult))
                order.then(dve.tensor_tensor(att[:], att[:], bo_all[:].unsqueeze(1).to_broadcast([P, QT, D]), ALU.add))
                dve.tensor_tensor(mine, mine, att[:], ALU.add).then_inc(h_ready, 1)
                assert order.n == ND2

            def low_q(b, g, par):
                dve.wait_ge(qh_ready, b * G + g + 1)
                dve.scalar_tensor_tensor(out=q1[D:P, par, :], in0=ps_m[D:P, :], scalar=bq2[D:P, :],
                                         in1=q1[D:P, par, :].bitcast(F32), op0=ALU.add, op1=ALU.subtract)
                dve.tensor_scalar(live_q[D:D + 1, par, :], ps_m[D:D + 1, :], bq2[D:D + 1, :], 0.0,
                                  ALU.add, ALU.not_equal).then_inc(q_ready, 1)

            def new_live(b, g, par):
                dve.wait_ge(q_ready, b * G + g + 1)
                dve.scalar_tensor_tensor(out=live[D:D + 1, par, :], in0=kh[D:D + 1, bass.ds(g * GQ, GQ)].bitcast(F32), scalar=0.0,
                                         in1=live_q[D:D + 1, par, :], op0=ALU.not_equal, op1=ALU.mult)

            def finish(b):
                order = Order(dve, s_dve3, b * ND3)
                wait_apart(dve, h_ready, G * (b + 1))
                layer_norm(order, h[:, bass.ds(b * N, N), :], b, 1)
                wts = weight[:, bass.ds(b * N, N)]

                def over_e(v):
                    return v.unsqueeze(2).to_broadcast([P, N, E])

                def over_n(v):
                    return v.unsqueeze(1).to_broadcast([P, N, E])

                dve.wait_ge(lg_full, b + 1)
                order.then(dve.tensor_tensor(lg[:], ps_m[:, 0:N * E].rearrange("p (n e) -> p n e", e=E),
                                             over_n(gb_all[:]), ALU.add))
                order.then(dve.tensor_reduce(rt[:, 0, :], lg[:], AX.X, ALU.max))
                order.then(dve.tensor_tensor(oneh[:], lg[:], over_e(rt[:, 0, :]), ALU.is_equal))
                order.then(dve.tensor_tensor(oneh[:], oneh[:], over_n(e_down[:]), ALU.mult))
                order.then(dve.tensor_reduce(rt[:, 1, :], oneh[:], AX.X, ALU.max))
                order.did(dve.tensor_tensor(oneh[:], oneh[:], over_e(rt[:, 1, :]), ALU.is_equal))
                dve.tensor_tensor(lg[:], lg[:], over_e(rt[:, 0, :]), ALU.subtract).then_inc(lg_centred, 1)
                dve.wait_ge(lg_exp, b + 1)
                order.then(dve.tensor_reduce(rt[:, 2, :], cum[:, 0, :, :], AX.X, ALU.add))
                order.did(dve.reciprocal(rt[:, 3, :], rt[:, 2, :]))
                order.then(dve.tensor_copy(cum[:, 0, :, :], oneh[:]))
                src = 0
                for s in (1, 2, 4, 8, 16):
                    order.did(dve.tensor_copy(cum[:, 1 - src, 0:s, :], cum[:, src, 0:s, :]))
                    ins = dve.tensor_tensor(cum[:, 1 - src, s:N, :], cum[:, src, s:N, :], cum[:, src, 0:N - s, :], ALU.add)
                    src = 1 - src
                    if s < 16:
                        order.then(ins)
                    else:
                        ins.then_inc(cp_ready, 1)
                dve.wait_ge(cb_full, b + 1)
                order.did(dve.tensor_tensor(carry[:], carry[:], cum[:, 1, N - 1, :], ALU.add))
                order.then(dve.tensor_copy(cbase[:], ps_m[:, N * E:(N + 1) * E]))
                order.then(dve.tensor_tensor(cum[:, 0, :, :], cum[:, 1, :, :], over_n(cbase[:]), ALU.add))
                order.then(dve.tensor_tensor(cum[:, 0, :, :], cum[:, 0, :, :], oneh[:], ALU.mult))
                order.did(dve.tensor_reduce(rt[:, 4, :], cum[:, 0, :, :], AX.X, ALU.add))
                order.then(dve.tensor_tensor(oneh[:], oneh[:], over_n(e_base[:]), ALU.mult))
                order.then(dve.tensor_reduce(rt[:, 5, :], oneh[:], AX.X, ALU.add))
                order.then(dve.tensor_scalar(rt[:, 0, :], rt[:, 4, :], float(CAP), None, ALU.is_le))
                order.did(dve.tensor_tensor(wts, rt[:, 3, :], rt[:, 0, :], ALU.mult))
                order.did(dve.tensor_scalar(rt[:, 1, :], rt[:, 0, :], -4.0 * E * CAP, 4.0 * E * CAP, ALU.mult, ALU.add))
                order.then(dve.tensor_scalar(rt[:, 2, :], rt[:, 4, :], float(CAP), -1.0, ALU.min, ALU.add))
                order.then(dve.tensor_tensor(rt[:, 2, :], rt[:, 2, :], rt[:, 5, :], ALU.add))
                dve.tensor_copy(get_at[:, bass.ds(b * N, N)], rt[:, 2, :])
                dve.tensor_tensor(put_at[:], rt[:, 2, :], rt[:, 1, :], ALU.add).then_inc(put_ready, 1)
                assert order.n == ND3, order.n

            images(dve, prepare, group, finish)

            with dve.Fori(0, E // 2) as pair:
                for par in range(2):
                    for a in range(CH):
                        c = par * CH + a
                        k = pair * (2 * CH) + c
                        e = pair * 2 + par
                        dve.wait_ge(hid_full, (k + 1) * 2)
                        dve.tensor_scalar(hid[:, 1, :], ps_s[:, 2, :],
                                          b1c[:, bass.ds(e, 1), 1:2].rearrange("p a b -> p (a b)"), 0.0,
                                          ALU.add, ALU.max).then_inc(hid_b, 1)
                        dve.wait_ge(yT_full, k + 1)
                        dve.tensor_scalar(yT, ps_s[0:D, 3, :], b2c[:, bass.ds(e, 1)], None, ALU.add).then_inc(yT_ready, 1)

            order = Order(dve, s_dve4, 0)
            for b in range(B):
                yg = (xn, xcen)[b % 2]
                tgt = h[:, b * N:(b + 1) * N, :]
                scr = p32[:, 0:2, :].rearrange("p a (n d) -> p (a n) d", d=D)
                dve.wait_ge(got, 16 * N * (b + 1))
                order.then(dve.tensor_tensor(yg[:], yg[:], spread(weight[:, b * N:(b + 1) * N]), ALU.mult))
                order.then(dve.tensor_scalar(scr, yg[:], 0.0, None, ALU.min))
                order.then(dve.scalar_tensor_tensor(out=yg[:], in0=yg[:], scalar=0.0, in1=scr, op0=ALU.max, op1=ALU.add))
                order.then(dve.tensor_scalar(scr, yg[:], 1e4, -1e4, ALU.min, ALU.max))
                order.then(dve.tensor_scalar(bad, yg[:], 0.0, 0.0, ALU.mult, ALU.not_equal))
                order.then(dve.copy_predicated(out=yg[:], mask=bad, data=scr))
                dve.tensor_tensor(tgt, tgt, yg[:], ALU.add).then_inc(out_ready, 1)


_INS = ['x', 'L0_tok_conv1_w', 'L0_tok_conv1_b', 'L0_tok_bn_gamma', 'L0_tok_bn_beta', 'L0_tok_bn_mean',
        'L0_tok_bn_var', 'L0_tok_conv2_w', 'L0_tok_conv2_b', 'L0_attn_Wq', 'L0_attn_bq', 'L0_attn_Wk', 'L0_attn_bk',
        'L0_attn_Wv', 'L0_attn_bv', 'L0_attn_Wo', 'L0_attn_bo', 'L0_ffn_gate_w', 'L0_ffn_gate_b', 'L0_ffn_w1',
        'L0_ffn_b1', 'L0_ffn_w2', 'L0_ffn_b2']


def kernel(**inputs):
    import concourse.bacc as _bacc
    from concourse.bass_utils import run_bass_kernel_spmd as _run

    nc = _bacc.Bacc("TRN2", target_bir_lowering=False, num_devices=1)
    arrays, args = {}, []
    for name in _INS:
        a = np.ascontiguousarray(inputs[name])
        arrays[f"in_{name}"] = a
        args.append(nc.dram_tensor(f"in_{name}", a.shape, mybir.dt.from_np(a.dtype), kind="ExternalInput").ap())
    b, c, hh, ww = inputs['x'].shape
    slots = -(-5 * b * c * hh // 4)
    args.append(nc.dram_tensor("out_0", (b, c * hh, ww), F32, kind="ExternalOutput").ap())
    args.append(nc.dram_tensor("slots_x", (slots, ww), F32).ap())
    args.append(nc.dram_tensor("slots_y", (slots, ww), F32).ap())
    tower(nc, *args)
    r = _run(nc, [arrays], core_ids=[0])
    return r.results[0]["out_0"]
```

```python
from contextlib import ExitStack

import numpy as np
import concourse.bass as bass
from concourse import mybir

F32 = mybir.dt.float32
F32R = mybir.dt.float32r
F16 = mybir.dt.float16
I32 = mybir.dt.int32
ALU = mybir.AluOpType
ACT = mybir.ActivationFunctionType
AX = mybir.AxisListType

P = 128
LN_EPS = 1e-5
BN_EPS = 1e-5


class Order:

    def __init__(self, eng, sem, base):
        self.eng, self.sem, self.base, self.n = eng, sem, base, 0

    def did(self, ins):
        ins.then_inc(self.sem, 1)
        self.n += 1
        return self.n

    def need(self, n):
        self.eng.wait_ge(self.sem, self.base + n)

    def then(self, ins):
        self.need(self.did(ins))


def tower(nc, x, conv1_w, conv1_b, bn_gamma, bn_beta, bn_mean, bn_var, conv2_w, conv2_b,
          Wq, bq, Wk, bk, Wv, bv, Wo, bo, gate_w, gate_b, w1, b1, w2, b2, out, slots_x):
    B, C, HH, WW = x.shape
    CR = conv1_w.shape[0]
    TAPS = conv2_w.shape[0]
    D = WW
    S = C * HH
    N = S // P
    RH = HH // 2
    E = gate_w.shape[1]
    F = w1.shape[2]
    CAP = -(-5 * B * S // (4 * E))
    GQ = 512
    G = S // GQ
    QT = GQ // P
    KC = S // 512
    STEPS = N // 2
    SCALE = float(D) ** -0.5
    LIFT = 8.0 * float(np.log(2.0)) / SCALE
    assert (B, C, HH, WW, CR, TAPS, E, F) == (4, 64, 64, 64, 16, 9, 8, 256)
    HALF = RH * WW
    PCH = HALF // 512
    FC = F // P
    CH = CAP // 512
    assert CH * 512 == CAP
    CENTER_FIRST = [4, 0, 1, 2, 3, 5, 6, 7, 8]
    FR = 20
    NOBODY = float(2 ** 20)
    LAG = 3
    RP = 4
    R32 = 3
    XR = CH

    with ExitStack() as ctx:
        ctx.enter_context(nc.allow_non_contiguous_dma(reason="small weights, loaded once"))
        def sb(name, shape, dt=F32):
            return ctx.enter_context(nc.sbuf_tensor(name, shape, dt))

        def psum(name, shape):
            return ctx.enter_context(nc.psum_tensor(name, shape, F32))

        def sem(name):
            return ctx.enter_context(nc.semaphore(name))

        out_rows = out.rearrange("b s d -> (b s) d")

        ps_s = psum("ps_s", [P, 4, 512])
        ps_a = psum("ps_a", [P, 2, 512])
        ps_o = psum("ps_o", [P, 512])
        ps_m = psum("ps_m", [P, 512])

        ident = sb("ident", [P, P])
        before = sb("before", [P, P])
        ones = sb("ones", [P, P])
        w_nat = sb("w_nat", [D, 4, 2, D])
        wq_t = sb("wq_t", [P, 2, D])
        wk_t = sb("wk_t", [P, 2, D])
        wq_p = sb("wq_p", [P, 2, P], F32R)
        wk_p = sb("wk_p", [P, 2, P], F32R)
        woT = sb("woT", [D, D])
        wvx = sb("wvx", [D, P])
        wg = sb("wg", [P, D + 2])
        bq2 = sb("bq2", [P, 1])
        bk2 = sb("bk2", [P, 1])
        bo_all = sb("bo_all", [P, D])
        w1bd = sb("w1bd", [P, P])
        bn_raw = sb("bn_raw", [P, 5])
        bn_t = sb("bn_t", [P, 4])
        bn_scale = sb("bn_scale", [P, 1])
        bn_bias = sb("bn_bias", [P, 1])
        cw2 = sb("cw2", [P, TAPS])
        tapw = sb("tapw", [P, 2, TAPS, C, 2], F32R)
        gw = sb("gw", [P, E])
        gw_p = sb("gw_p", [P, 2, E], F32R)
        gb_all = sb("gb_all", [P, E])
        e_down = sb("e_down", [P, E])
        e_base = sb("e_base", [P, E])
        b1c = sb("b1c", [P, E, FC])
        b2c = sb("b2c", [D, E])

        xh = sb("xh", [P, RH + 2, WW])
        xc = sb("xc", [P, HALF])
        y = sb("y", [P, 2, 512], F32R)
        y32 = sb("y32", [P, 512])
        tmp = sb("tmp", [P, 2, 8, WW])
        h = sb("h", [P, 2 * N, D])
        xcen = sb("xcen", [P, N, D])
        xhl = sb("xhl", [P, N, 2, D])
        fill = xcen[:].rearrange("p n d -> p (n d)")[:, 0:FR * (D + 2)].rearrange("p (a d) -> p a d", a=FR)
        ln_s = sb("ln_s", [P, 6, N])
        xs = sb("xs", [P, N, P], F16)
        xT = sb("xT", [P, S], F32R)
        kh = sb("kh", [P, S], F32R)
        kl = sb("kl", [P, S], F32R)
        q1 = sb("q1", [P, 2, GQ], F32R)
        q2 = sb("q2", [P, 2, GQ], F32R)
        own = sb("own", [D + QT, QT, P])
        live_q = sb("live_q", [65, GQ])
        live = sb("live", [65, 2, GQ])
        mx = sb("mx", [P, QT, KC])
        rowmax = sb("rowmax", [P, QT])
        p32 = sb("p32", [P, R32, 1024])
        ph = sb("ph", [P, RP, 1024], F16)
        pl = sb("pl", [P, RP, 1024], F16)
        oT = sb("oT", [P, GQ])
        post = sb("post", [P, 2, QT])
        att = sb("att", [P, QT, D])

        lg = sb("lg", [P, N, E])
        rt = sb("rt", [P, 6, N])
        oneh = sb("oneh", [P, N, E])
        cum = sb("cum", [P, 2, N, E])
        carry = sb("carry", [P, E])
        cbase = sb("cbase", [P, E])
        xw = sb("xw", [P, N, D + 2])
        token = sb("token", [P, N])
        put_at = sb("put_at", [P, N], I32)

        w1s = sb("w1s", [P, F])
        w1p = sb("w1p", [P, 2, 2, F], F32R)
        w2s = sb("w2s", [P, 2, FC, D])
        add_at = sb("add_at", [P, 2, 4], I32)
        xm = xcen[:].rearrange("p n d -> p (n d)")[:, 0:XR * 4 * (D + 2)].rearrange("p (c a d) -> p c a d", c=XR, a=4)
        ym = p32[:, 2, 0:8 * D].rearrange("p (c a d) -> p c a d", c=2, a=4)
        xmhl = p32[:, 2, 8 * D:16 * D].rearrange("p (a t d) -> p a t d", a=4, t=2)
        yscr = att[:]
        bad = lg[:].rearrange("p (a n) e -> p a (n e)", a=4).bitcast(I32)
        xmT = xT[:, 0:1024].rearrange("p (c s) -> p c s", c=2)
        yT = (oT[0:D, :], y32[0:D, :])
        hid = p32[:, 0:2, :].rearrange("p c (f s) -> p c f s", f=FC)

        consts_in = sem("consts_in")
        zero_out = sem("zero_out")
        made = sem("made")
        cleared = sem("cleared")
        s_dset = sem("s_dset")
        s_pset = sem("s_pset")
        s_aset = sem("s_aset")
        x_in = sem("x_in")
        x_free = sem("x_free")
        conv1 = sem("conv1")
        y_high = sem("y_high")
        y_ready = sem("y_ready")
        tap_full = sem("tap_full")
        tap_used = sem("tap_used")
        s_dve1 = sem("s_dve1")
        var_ready = sem("var_ready")
        sd_ready = sem("sd_ready")
        xn_ready = sem("xn_ready")
        xt_full = sem("xt_full")
        xt_ready = sem("xt_ready")
        k_full = sem("k_full")
        kh_ready = sem("kh_ready")
        kl_ready = sem("kl_ready")
        xs_ready = sem("xs_ready")
        q_full = sem("q_full")
        qh_ready = sem("qh_ready")
        q_ready = sem("q_ready")
        a_full = sem("a_full")
        a_used = sem("a_used")
        max_ready = sem("max_ready")
        mrow_full = sem("mrow_full")
        mrow_ready = sem("mrow_ready")
        s_full = sem("s_full")
        ph_ready = sem("ph_ready")
        pl_ready = sem("pl_ready")
        av_done = sem("av_done")
        oT_ready = sem("oT_ready")
        live_in = sem("live_in")
        post_full = sem("post_full")
        s_dve2 = sem("s_dve2")
        h_ready = sem("h_ready")
        lg_full = sem("lg_full")
        lg_centred = sem("lg_centred")
        lg_exp = sem("lg_exp")
        s_dve3 = sem("s_dve3")
        cp_ready = sem("cp_ready")
        cb_full = sem("cb_full")
        put_ready = sem("put_ready")
        put_done = sem("put_done")
        xn_free = sem("xn_free")
        w_in = sem("w_in")
        w_free = sem("w_free")
        w_ready = sem("w_ready")
        xm_in = [sem(f"xm_in{i}") for i in range(XR)]
        xmT_full = sem("xmT_full")
        xmhl_ready = sem("xmhl_ready")
        xmT_ready = sem("xmT_ready")
        hid_full = sem("hid_full")
        hid_a = sem("hid_a")
        hid_b = sem("hid_b")
        yT_full = sem("yT_full")
        yT_ready = sem("yT_ready")
        ym_full = sem("ym_full")
        ym_read = sem("ym_read")
        ym_ready = sem("ym_ready")
        y_out = [sem("y_out0"), sem("y_out1")]
        s_dve4 = sem("s_dve4")
        stored = sem("stored")
        waits = {e.engine: sem(f"waits_{n}") for n, e in (("pe", nc.tensor), ("act", nc.scalar),
                                                          ("dve", nc.vector), ("pool", nc.gpsimd),
                                                          ("sp", nc.sync))}

        def wait_apart(eng, semaphore, value):
            eng.wait_ge(semaphore, value)
            eng.sem_inc(waits[eng.engine], 1)

        def images(eng, prepare, group, finish):
            with eng.Fori(0, B) as b:
                prepare(b)
                with eng.Fori(0, G // 2 - 1) as pair:
                    group(b, pair * 2, 0, False)
                    group(b, pair * 2 + 1, 1, False)
                group(b, G - 2, 0, False)
                group(b, G - 1, 1, True)
                finish(b)

        def has_query_product(g):
            return not (isinstance(g, int) and g + 2 >= G)

        def step0(b, g):
            return (b * G + g) * STEPS

        FILLS = E * CAP // (FR * P)
        N_CONST = 10 + 4 * 8 + 2 + 5
        ND1 = PCH * TAPS + 9
        ND2 = 4
        ND3 = 41
        ND4 = 2 * 2 + 2 * CH * 5

        block = ctx.enter_context(nc.Block())

        @block.sync
        def _(sp):
            for i, w in enumerate((Wq, Wk, Wv, Wo)):
                for t in range(2 if i < 2 else 1):
                    sp.dma_start(w_nat[:, i, t, :], w).then_inc(consts_in, 16)
            for dst, v in ((bq2, bq), (bk2, bk)):
                for half in range(2):
                    sp.dma_start(dst[D * half:D * (half + 1), :], v.rearrange("(a b) -> a b", b=1)).then_inc(consts_in, 16)
            sp.wait_ge(made, 4)
            for low in range(2):
                for half in range(2):
                    row = 64 * low + 32 * half
                    sp.dma_start(w1bd[C * half:C * (half + 1), row:row + CR],
                                 conv1_w.rearrange("o c -> c o")).then_inc(consts_in, 16)
                    for i, v in enumerate((conv1_b, bn_gamma, bn_beta, bn_mean, bn_var)):
                        sp.dma_start(bn_raw[row:row + CR, i:i + 1],
                                     v.rearrange("(a b) -> a b", b=1)).then_inc(consts_in, 16)
                    sp.dma_start(cw2[row:row + CR, :], conv2_w.rearrange("k o -> o k")).then_inc(consts_in, 16)
                    sp.dma_start(cw2[row + CR:row + CR + 1, :],
                                 conv2_b.rearrange("(b a) -> b a", b=1)).then_inc(consts_in, 16)
                sp.dma_start(gw[D * low:D * (low + 1), :], gate_w).then_inc(consts_in, 16)
            sp.dma_start(wvx[:, 63:64], bv.rearrange("(a b) -> a b", b=1)).then_inc(consts_in, 16)
            sp.dma_start(bo_all[:], bo.partition_broadcast(P)).then_inc(consts_in, 16)
            sp.dma_start(gb_all[:], gate_b.partition_broadcast(P)).then_inc(consts_in, 16)
            sp.dma_start(b1c[:], b1.rearrange("e (f p) -> p e f", p=P)).then_inc(consts_in, 16)
            sp.dma_start(b2c[:], b2.rearrange("e d -> d e")).then_inc(consts_in, 16)

            sp.wait_ge(cleared, 1)
            with sp.Fori(0, B) as b:
                sp.wait_ge(x_free, b + 1)
                for half in range(2):
                    lo = 0 if half == 0 else RH - 1
                    sp.dma_start(
                        xh[half:P:2, 1 - half:RH + 2 - half, :],
                        x[bass.ds(b, 1), :, lo:lo + RH + 1, :].rearrange("a c r w -> (a c) r w")).then_inc(x_in, 16)
                    sp.dma_start(
                        xc[C * half:C * (half + 1), :],
                        x[bass.ds(b, 1), :, RH * half:RH * (half + 1), :].rearrange("a c r w -> (a c) (r w)"),
                    ).then_inc(x_in, 16)

                wait_apart(sp, h_ready, G * (b + 1))
                sp.dma_start(out[bass.ds(b, 1)].rearrange("a (p n) d -> p (a n) d", p=P),
                             h[:, bass.ds(b % 2 * N, N), :]).then_inc(stored, 16)
                wait_apart(sp, stored, (b + 1) * 16)

            with sp.Fori(0, E // 2) as pair:
                for par in range(2):
                    sp.wait_ge(w_free, pair * 2 + par + 1)
                    e = pair * 2 + par
                    for low in range(2):
                        sp.dma_start(w1s[D * low:D * (low + 1), :],
                                     w1[bass.ds(e, 1)].rearrange("a d f -> (a d) f")).then_inc(w_in, 16)
                    sp.dma_start(w2s[:, par, :, :],
                                 w2[bass.ds(e, 1)].rearrange("a (f p) d -> p (a f) d", p=P)).then_inc(w_in, 16)
                    for a in range(CH):
                        c = par * CH + a
                        k = pair * (2 * CH) + c
                        if c < XR:
                            sp.wait_ge(put_done, 16 * N * B)
                        sp.wait_ge(ym_read, k + 1)
                        sp.dma_start(xm[:, c % XR, :, :],
                                     slots_x[bass.ds(k * 512, 512), :].rearrange("(p a) d -> p a d", p=P),
                                     ).then_inc(xm_in[c % XR], 16)
            sp.wait_ge(stored, 16 * B)
            sp.wait_ge(zero_out, 16 * FILLS)

        @block.gpsimd
        def _(pool):
            pool.sem_inc(xn_free, 1)
            pool.memset(bn_raw[:], 0.0).then_inc(made, 1)
            pool.memset(w1bd[:], 0.0).then_inc(made, 1)
            pool.memset(wvx[:], 0.0).then_inc(made, 1)
            pool.memset(cw2[:], 0.0).then_inc(made, 1)
            pool.memset(ones[:], 1.0).then_inc(made, 1)
            pool.memset(fill[:, :, 0:D + 1], 0.0)
            pool.memset(fill[:, :, D + 1:D + 2], NOBODY).then_inc(made, 1)
            pool.wait_ge(made, 6)
            pool.affine_select(out=ident[:], in_=ones[:], compare_op=ALU.is_equal, fill=0.0, base=0,
                               pattern=[[1, P]], channel_multiplier=-1).then_inc(made, 1)
            pool.affine_select(out=before[:], in_=ones[:], compare_op=ALU.is_gt, fill=0.0, base=0,
                               pattern=[[1, P]], channel_multiplier=-1).then_inc(made, 1)
            pool.iota(token[:], pattern=[[1, N]], base=0, channel_multiplier=N,
                      allow_small_or_imprecise_dtypes=True).then_inc(made, 1)
            pool.iota(e_down[:], pattern=[[-1, E]], base=E, channel_multiplier=0,
                      allow_small_or_imprecise_dtypes=True).then_inc(made, 1)
            pool.iota(e_base[:], pattern=[[CAP, E]], base=0, channel_multiplier=0,
                      allow_small_or_imprecise_dtypes=True).then_inc(made, 1)

            def prepare(b):
                pass

            def group(b, g, par, last):
                t0 = step0(b, g)
                for j in range(STEPS):
                    pool.wait_ge(ph_ready, t0 + j + 1)
                    pool.tensor_tensor(out=pl[:, j % RP, :], in0=p32[:, j % R32, :], in1=ph[:, j % RP, :],
                                       op=ALU.subtract).then_inc(pl_ready, 1)

            def finish(b):
                pool.wait_ge(zero_out, 16 * FILLS)
                wait_apart(pool, put_ready, b + 1)
                for n in range(N):
                    pool.indirect_dma_start(slots_x, bass.IndirectOffsetOnAxis(ap=put_at[:, n:n + 1], axis=0),
                                            xw[:, n, :], None, bounds_check=E * CAP - 1,
                                            oob_is_err=False).then_inc(put_done, 16)
                pool.wait_ge(put_done, (b + 1) * (16 * N))
                pool.sem_inc(xn_free, 1)

            images(pool, prepare, group, finish)

            pool.wait_ge(stored, 16 * B)
            with pool.Fori(0, E // 2) as pair:
                for c in range(2 * CH):
                    k = pair * (2 * CH) + c
                    wait_apart(pool, ym_ready, k + 1)
                    for a in range(4):
                        pool.indirect_dma_start(out_rows, bass.IndirectOffsetOnAxis(ap=add_at[:, c % 2, a:a + 1], axis=0),
                                                ym[:, c % 2, a, :], None, bounds_check=B * S - 1, oob_is_err=False,
                                                compute_op=ALU.add).then_inc(y_out[c % 2], 16)
            pool.wait_ge(y_out[0], 16 * 4 * E * CH // 2)
            pool.wait_ge(y_out[1], 16 * 4 * E * CH // 2)

        @block.tensor
        def _(pe):
            pe.wait_ge(made, 8)
            pe.wait_ge(consts_in, 16 * N_CONST)
            for i in range(2):
                pe.transpose(ps_m[:, D * i:D * (i + 1)], w_nat[:, i, :, :].rearrange("o t w -> o (t w)"), ident[0:D, 0:D])
            pe.transpose(ps_m[0:D, 2 * D:3 * D], w_nat[:, 3, 0, :], ident[0:D, 0:D]).then_inc(s_pset, 1)
            pe.wait_ge(s_dset, 1)
            pe.matmul(ps_m[:, 256:256 + D], wvx[:], woT[:], start=True, stop=True).then_inc(s_pset, 1)

            def q_product(b, g):
                for part in range(2):
                    mm = pe.matmul(ps_m[:], wq_p[:, part, :], xT[:, bass.ds(g * GQ, GQ)], start=(part == 0),
                                   stop=(part == 1))
                mm.then_inc(q_full, 1)

            def a_product(b, g, par, a):
                if a == 0:
                    pe.wait_ge(q_ready, b * G + g + 1)
                if a >= 2:
                    pe.wait_ge(a_used, (b * G + g) * (QT * KC) + a - 1)
                qt, kc = a // KC, a % KC
                pe.matmul(ps_a[:, a % 2, :], q1[:, par, qt * P:(qt + 1) * P], kh[:, kc * 512:(kc + 1) * 512],
                          start=True, stop=True).then_inc(a_full, 1)

            def max_rows(b, g):
                pe.wait_ge(max_ready, b * G + g + 1)
                pe.matmul(ps_m[D:D + QT, 0:P], rowmax[:], ident[:], start=True, stop=True).then_inc(mrow_full, 1)

            def prepare(b):
                pe.wait_ge(x_in, 64 * (b + 1))
                for i in range(PCH):
                    pe.matmul(ps_s[:, i, :], w1bd[:], xc[:, i * 512:(i + 1) * 512],
                              start=True, stop=True).then_inc(conv1, 1)
                for i in range(PCH):
                    pe.wait_ge(y_ready, PCH * b + i + 1)
                    for kk, k in enumerate(CENTER_FIRST):
                        t = i * TAPS + kk
                        if t >= 2:
                            pe.wait_ge(tap_used, PCH * TAPS * b + t - 1)
                        for part in range(2):
                            mm = pe.matmul(ps_a[:, t % 2, :], tapw[:, part, k, :, :], y[:, i % 2, :],
                                           start=(part == 0), stop=(part == 1))
                        mm.then_inc(tap_full, 1)
                transposed(b, 0)
                for c in range(KC):
                    if c >= 2:
                        pe.wait_ge(kl_ready, KC * b + c - 1)
                    for part in range(2):
                        mm = pe.matmul(ps_a[:, c % 2, :], wk_p[:, part, :], xT[:, c * 512:(c + 1) * 512],
                                       start=(part == 0), stop=(part == 1))
                    mm.then_inc(k_full, 1)
                q_product(b, 0)
                pe.wait_ge(kl_ready, KC * (b + 1))
                for a in range(QT * KC):
                    a_product(b, 0, 0, a)
                max_rows(b, 0)
                pe.wait_ge(mrow_ready, b * G + 1)
                q_product(b, 1)

            def transposed(b, which):
                wait_apart(pe, xn_ready, 2 * b + which + 1)
                for c in range(KC):
                    if c >= 4:
                        wait_apart(pe, xt_ready, (2 * b + which) * KC + c - 3)
                    for i in range(4):
                        mm = pe.transpose(ps_s[:, c % 4, i * P:(i + 1) * P],
                                          xhl[:, 4 * c + i, :, :].rearrange("p t d -> p (t d)"), ident[:])
                    mm.then_inc(xt_full, 1)
                pe.wait_ge(xt_ready, (2 * b + which + 1) * KC)

            def group(b, g, par, last):
                t0 = step0(b, g)

                def scores(j):
                    if j == 0:
                        pe.wait_ge(mrow_ready, b * G + g + 1)
                    if j >= 2:
                        pe.wait_ge(ph_ready, t0 + j - 1)
                    for i in range(2):
                        n = 2 * j + i
                        dst = ps_s[:, 2 * (j % 2) + i, :]
                        pe.matmul(dst, kh[:, n * P:(n + 1) * P], q1[:, par, :], start=True, stop=False)
                        mm = pe.matmul(dst, kl[:, n * P:(n + 1) * P], q2[:, par, :], start=False, stop=True)
                    mm.then_inc(s_full, 1)

                def weigh(j):
                    pe.wait_ge(ph_ready, t0 + j + 1)
                    for i in range(2):
                        pe.matmul(ps_o[:], xs[:, 2 * j + i, :], ph[:, j % RP, i * 512:(i + 1) * 512],
                                  start=(j == 0 and i == 0), stop=False)
                    pe.wait_ge(pl_ready, t0 + j + 1)
                    for i in range(2):
                        mm = pe.matmul(ps_o[:], xs[:, 2 * j + i, :], pl[:, j % RP, i * 512:(i + 1) * 512],
                                       start=False, stop=(j == STEPS - 1 and i == 1))
                    mm.then_inc(av_done, 1)

                a = 0
                for j in range(STEPS + LAG):
                    if j < STEPS:
                        scores(j)
                    if not last:
                        for _ in range(3):
                            if j >= 1 and a < QT * KC:
                                a_product(b, g + 1, 1 - par, a)
                                a += 1
                        if j == 13:
                            max_rows(b, g + 1)
                    if j == STEPS and not last:
                        pe.wait_ge(mrow_ready, b * G + g + 2)
                        if has_query_product(g):
                            q_product(b, g + 2)
                    if j >= LAG:
                        weigh(j - LAG)
                pe.wait_ge(live_in, b * G + g + 1)
                if has_query_product(g):
                    pe.wait_ge(q_ready, b * G + g + 3)
                for qt in range(QT):
                    mm = pe.matmul(ps_m[:, qt * (D + 2):(qt + 1) * (D + 2)], oT[:, qt * P:(qt + 1) * P], wg[:],
                                   start=True, stop=True)
                mm.then_inc(post_full, 1)
                pe.wait_ge(h_ready, b * G + g + 1)

            def finish(b):
                transposed(b, 1)
                for n in range(N):
                    mm = pe.matmul(ps_m[:, n * 2 * E:(n + 1) * 2 * E], xT[:, n * P:(n + 1) * P], gw_p[:],
                                   start=True, stop=True)
                mm.then_inc(lg_full, 1)
                pe.wait_ge(cp_ready, b + 1)
                pe.matmul(ps_a[:, 0, 0:E], before[:], cum[:, 1, N - 1, :], start=True, stop=False)
                pe.matmul(ps_a[:, 0, 0:E], ones[:], carry[:], start=False, stop=True).then_inc(cb_full, 1)

            images(pe, prepare, group, finish)

            with pe.Fori(0, E // 2) as pair:
                def turn_in(c):
                    k = pair * (2 * CH) + c
                    wait_apart(pe, xmhl_ready, k + 1)
                    for i in range(4):
                        mm = pe.transpose(ps_a[:, c % 2, i * P:(i + 1) * P],
                                          xmhl[:, i, :, :].rearrange("p t d -> p (t d)"), ident[:])
                    mm.then_inc(xmT_full, 1)

                def hidden(c):
                    k = pair * (2 * CH) + c
                    if c % CH == 0:
                        pe.wait_ge(w_ready, pair * 2 + c // CH + 1)
                    pe.wait_ge(xmT_ready, k + 1)
                    for f in range(FC):
                        for part in range(2):
                            mm = pe.matmul(ps_s[:, 2 * (c % 2) + f, :], w1p[:, c // CH, part, f * P:(f + 1) * P],
                                           xmT[:, c % 2, :], start=(part == 0), stop=(part == 1))
                        mm.then_inc(hid_full, 1)

                def result(c):
                    k = pair * (2 * CH) + c
                    pe.wait_ge(hid_a, k + 1)
                    pe.wait_ge(hid_b, k + 1)
                    for f in range(FC):
                        mm = pe.matmul(ps_o[0:D, :], w2s[:, c // CH, f, :], hid[:, c % 2, f, :],
                                       start=(f == 0), stop=(f == 1))
                    mm.then_inc(yT_full, 1)

                def turn_out(c):
                    k = pair * (2 * CH) + c
                    wait_apart(pe, yT_ready, k + 1)
                    wait_apart(pe, ym_read, k + XR)
                    for i in range(4):
                        mm = pe.transpose(ps_m[:, i * D:(i + 1) * D], yT[c % 2][:, i * P:(i + 1) * P], ident[0:D, 0:D])
                    mm.then_inc(ym_full, 1)

                turn_in(0)
                for c in range(2 * CH):
                    hidden(c)
                    if c + 1 < 2 * CH:
                        turn_in(c + 1)
                    if c >= 1:
                        turn_out(c - 1)
                    result(c)
                turn_out(2 * CH - 1)

        @block.scalar
        def _(act):
            act.wait_ge(made, 6)
            for q in range(FILLS):
                act.dma_start(slots_x[q * FR * P:(q + 1) * FR * P, :].rearrange("(p a) d -> p a d", p=P),
                              fill).then_inc(zero_out, 16)
            act.wait_ge(s_dset, 2)
            act.activation(bn_t[:, 1:2], bn_t[:, 0:1], ACT.Sqrt).then_inc(s_aset, 1)

            def root(b, which):
                act.wait_ge(var_ready, 2 * b + which + 1)
                act.activation(ln_s[:, 4, :], ln_s[:, 3, :], ACT.Sqrt).then_inc(sd_ready, 1)

            def take_xT(b, which):
                for c in range(KC):
                    act.wait_ge(xt_full, (2 * b + which) * KC + c + 1)
                    act.activation(xT[:, c * 512:(c + 1) * 512], ps_s[:, c % 4, :], ACT.Copy).then_inc(xt_ready, 1)

            def take_q(b, g, par):
                act.wait_ge(q_full, b * G + g + 1)
                act.activation(q2[0:D, par, :], ps_m[0:D, :], ACT.Identity, bias=bq2[0:D, :])
                act.activation(q1[:, par, :], ps_m[:], ACT.Identity, bias=bq2[:]).then_inc(qh_ready, 1)

            def prepare(b):
                for i in range(PCH):
                    act.wait_ge(conv1, PCH * b + i + 1)
                    if i == 0:
                        act.wait_ge(s_dset, 9)
                    if i >= 2:
                        act.wait_ge(tap_full, (PCH * b + i - 1) * TAPS)
                    act.activation(y[:, i % 2, :], ps_s[:, i, :], ACT.Relu,
                                   bias=bn_bias[:], scale=bn_scale[:]).then_inc(y_high, 1)
                root(b, 0)
                take_xT(b, 0)
                for c in range(KC):
                    act.wait_ge(k_full, KC * b + c + 1)
                    act.activation(kh[:, c * 512:(c + 1) * 512], ps_a[:, c % 2, :], ACT.Identity,
                                   bias=bk2[:]).then_inc(kh_ready, 1)
                take_q(b, 0, 0)
                take_q(b, 1, 1)

            def group(b, g, par, last):
                t0 = step0(b, g)
                for j in range(STEPS):
                    act.wait_ge(s_full, t0 + j + 1)
                    if j >= R32:
                        act.wait_ge(pl_ready, t0 + j - R32 + 1)
                    act.activation(p32[:, j % R32, :], ps_s[:, 2 * (j % 2):2 * (j % 2) + 2, :], ACT.Exp, scale=SCALE)
                    if j >= RP:
                        act.wait_ge(av_done, t0 + j - RP + 1)
                    act.activation(ph[:, j % RP, :], ps_s[:, 2 * (j % 2):2 * (j % 2) + 2, :], ACT.Exp,
                                   scale=SCALE).then_inc(ph_ready, 1)
                if has_query_product(g):
                    take_q(b, g + 2, par)
                act.wait_ge(av_done, t0 + STEPS)
                act.activation(oT[:], ps_o[:], ACT.Copy).then_inc(oT_ready, 1)

            def finish(b):
                root(b, 1)
                take_xT(b, 1)
                act.wait_ge(lg_centred, b + 1)
                act.activation(cum[:, 0, :, :], lg[:], ACT.Exp).then_inc(lg_exp, 1)

            images(act, prepare, group, finish)

            with act.Fori(0, E // 2) as pair:
                for c in range(2 * CH):
                    k = pair * (2 * CH) + c
                    act.wait_ge(xmT_full, k + 1)
                    act.activation(xmT[:, c % 2, :], ps_a[:, c % 2, :], ACT.Copy).then_inc(xmT_ready, 1)
                    wait_apart(act, hid_full, (k + 1) * 2 - 1)
                    if c >= 2:
                        wait_apart(act, yT_full, k - 1)
                    act.activation(hid[:, c % 2, 0, :], ps_s[:, 2 * (c % 2), :], ACT.Relu,
                                   bias=b1c[:, bass.ds(pair * 2 + c // CH, 1), 0:1].rearrange("p a b -> p (a b)")
                                   ).then_inc(hid_a, 1)

        @block.vector
        def _(dve):
            dve.memset(carry[:], 0.0)
            dve.memset(xh[:, 0:1, :], 0.0)
            dve.memset(xh[:, RH + 1:RH + 2, :], 0.0)
            dve.memset(kl[D:P, :].bitcast(F32), 0.0)
            dve.memset(q2[D:P, :, :].bitcast(F32), 0.0)
            tap32 = p32[:].rearrange("p a b -> p (a b)")[:, 0:TAPS * P].rearrange("p (k c h) -> p k c h", k=TAPS, h=2)
            dve.memset(xs[:], 0.0)
            dve.memset(tap32, 0.0).then_inc(cleared, 1)
            dve.wait_ge(cleared, 1)
            dve.memset(kl[D:D + QT, :].bitcast(F32), 1.0)
            dve.sem_inc(ym_read, XR)
            dve.sem_inc(w_free, 1)
            dve.sem_inc(x_free, 1)

            setup = Order(dve, s_dset, 0)
            dve.wait_ge(consts_in, 16 * N_CONST)
            dve.wait_ge(made, 11)
            dve.wait_ge(s_pset, 1)
            dve.tensor_copy(wq_t[:], ps_m[:, 0:D].unsqueeze(1).to_broadcast([P, 2, D]))
            dve.tensor_copy(wk_t[:], ps_m[:, D:2 * D].unsqueeze(1).to_broadcast([P, 2, D]))
            dve.tensor_copy(wg[:, D:D + 2], ident[:, 63:65])
            dve.tensor_scalar(own[D:D + QT, :, :], ident[D:D + QT, D:D + QT].unsqueeze(2).to_broadcast([QT, QT, P]),
                              -1.0, None, ALU.mult)
            dve.tensor_copy(woT[:], ps_m[0:D, 2 * D:3 * D])
            dve.tensor_scalar(wvx[:, 0:63], w_nat[:, 2, 0, 0:63], w_nat[:, 2, 0, 63:64], None, ALU.subtract)
            setup.did(dve.tensor_scalar(wvx[:, 65:128], w_nat[:, 2, 0, 0:63], w_nat[:, 2, 0, 63:64], None, ALU.subtract))
            dve.memset(xs[:, :, 63:64], 1.0)
            setup.did(dve.tensor_scalar(bn_t[:, 0:1], bn_raw[:, 4:5], BN_EPS, None, ALU.add))
            dve.tensor_tensor(bn_t[:, 3:4], bn_raw[:, 0:1], bn_raw[:, 3:4], ALU.subtract)
            setup.then(dve.tensor_tensor(bn_raw[:, 2:3], bn_raw[:, 2:3], ident[:, CR:CR + 1], ALU.add))
            setup.then(dve.tensor_tensor(bn_raw[:, 2:3], bn_raw[:, 2:3], ident[:, 32 + CR:33 + CR], ALU.add))
            dve.wait_ge(s_aset, 1)
            setup.then(dve.reciprocal(bn_t[:, 2:3], bn_t[:, 1:2]))
            setup.then(dve.tensor_tensor(bn_scale[:], bn_raw[:, 1:2], bn_t[:, 2:3], ALU.mult))
            for low in range(2):
                for half in range(2):
                    rows = slice(64 * low + 32 * half, 64 * low + 32 * half + CR + 1)
                    ins = dve.tensor_copy(tap32[rows, :, :, half],
                                          cw2[rows, :].unsqueeze(2).to_broadcast([CR + 1, TAPS, C]))
            setup.then(ins)
            dve.tensor_copy(tapw[:, 0], tap32)
            dve.tensor_copy(wq_p[:, 0, :], wq_t[:].rearrange("p a b -> p (a b)"))
            dve.tensor_copy(wk_p[:, 0, :], wk_t[:].rearrange("p a b -> p (a b)"))
            setup.then(dve.tensor_copy(gw_p[:, 0, :], gw[:]))
            dve.tensor_tensor(tapw[:, 1], tap32, tapw[:, 0].bitcast(F32), ALU.subtract)
            dve.tensor_tensor(wq_p[:, 1, :], wq_t[:].rearrange("p a b -> p (a b)"), wq_p[:, 0, :].bitcast(F32), ALU.subtract)
            dve.tensor_tensor(wk_p[:, 1, :], wk_t[:].rearrange("p a b -> p (a b)"), wk_p[:, 0, :].bitcast(F32), ALU.subtract)
            dve.tensor_tensor(gw_p[:, 1, :], gw[:], gw_p[:, 0, :].bitcast(F32), ALU.subtract)
            dve.scalar_tensor_tensor(out=bn_bias[:], in0=bn_t[:, 3:4], scalar=bn_scale[:], in1=bn_raw[:, 2:3],
                                     op0=ALU.mult, op1=ALU.add).then_inc(s_dset, 1)
            dve.wait_ge(s_pset, 2)
            dve.tensor_copy(wg[:, 0:D], ps_m[:, 256:256 + D]).then_inc(s_dset, 1)

            def spread(v):
                return v.unsqueeze(2).to_broadcast([P, N, D])

            def layer_norm(order, src, dst, b, which):
                order.then(dve.tensor_reduce(ln_s[:, 0, :], src, AX.X, ALU.add))
                order.then(dve.tensor_scalar(ln_s[:, 1, :], ln_s[:, 0, :], 1.0 / D, None, ALU.mult))
                order.then(dve.tensor_tensor(xcen[:], src, spread(ln_s[:, 1, :]), ALU.subtract))
                order.then(dve.tensor_tensor(xhl[:, :, 0, :], xcen[:], xcen[:], ALU.mult))
                order.then(dve.tensor_reduce(ln_s[:, 2, :], xhl[:, :, 0, :], AX.X, ALU.add))
                dve.tensor_scalar(ln_s[:, 3, :], ln_s[:, 2, :], 1.0 / D, LN_EPS, ALU.mult, ALU.add).then_inc(var_ready, 1)
                dve.wait_ge(sd_ready, 2 * b + which + 1)
                order.then(dve.reciprocal(ln_s[:, 5, :], ln_s[:, 4, :]))
                order.then(dve.tensor_tensor(dst, xcen[:], spread(ln_s[:, 5, :]), ALU.mult))
                order.then(dve.tensor_copy(xhl[:, :, 0, :].bitcast(F32R), dst))
                dve.tensor_tensor(xhl[:, :, 1, :].bitcast(F32R), dst, xhl[:, :, 0, :], ALU.subtract).then_inc(xn_ready, 1)

            def prepare(b):
                order = Order(dve, s_dve1, b * ND1)
                dve.wait_ge(x_in, 64 * (b + 1))
                def low_y(i):
                    if i >= 1:
                        dve.wait_ge(y_ready, PCH * b + i)
                    dve.wait_ge(y_high, PCH * b + i + 1)
                    order.then(dve.tensor_scalar(y32[D:P, :], ps_s[D:P, i, :], bn_scale[D:P, :], bn_bias[D:P, :],
                                                 ALU.mult, ALU.add))
                    dve.scalar_tensor_tensor(out=y[D:P, i % 2, :], in0=y32[D:P, :], scalar=0.0,
                                             in1=y[D:P, i % 2, :].bitcast(F32),
                                             op0=ALU.max, op1=ALU.subtract).then_inc(y_ready, 1)

                low_y(0)
                low_y(1)
                for i in range(PCH):
                    mine = h[:, bass.ds(b % 2 * N + 8 * i, 8), :]
                    for kk, k in enumerate(CENTER_FIRST):
                        t = i * TAPS + kk
                        dr, dc = k // 3, k % 3 - 1
                        w0, w1_ = max(0, -dc), min(WW, WW - dc)
                        wd = ps_a[:, t % 2, :].rearrange("p (r w) -> p r w", w=WW)[:, :, w0:w1_]
                        src = xh[:, 8 * i + dr:8 * i + dr + 8, w0 + dc:w1_ + dc]
                        dve.wait_ge(tap_full, PCH * TAPS * b + t + 1)
                        if kk == 0:
                            dve.tensor_tensor(mine, wd, src, ALU.mult).then_inc(tap_used, 1)
                            continue
                        dve.tensor_tensor(tmp[:, kk % 2, :, w0:w1_], wd, src, ALU.mult).then_inc(tap_used, 1)
                        dve.wait_ge(tap_used, PCH * TAPS * b + t + 1)
                        order.then(dve.tensor_tensor(mine[:, :, w0:w1_], mine[:, :, w0:w1_],
                                                     tmp[:, kk % 2, :, w0:w1_], ALU.add))
                    if i + 2 < PCH:
                        low_y(i + 2)
                dve.sem_inc(x_free, 1)
                dve.wait_ge(zero_out, 16 * FILLS)
                layer_norm(order, h[:, bass.ds(b % 2 * N, N), :], xcen[:], b, 0)
                order.then(dve.tensor_copy(xs[:, :, 0:63], xcen[:, :, 0:63]))
                dve.tensor_tensor(xs[:, :, 65:128], xcen[:, :, 0:63], xs[:, :, 0:63], ALU.subtract).then_inc(xs_ready, 1)
                assert order.n == ND1, order.n
                for c in range(KC):
                    dve.wait_ge(kh_ready, KC * b + c + 1)
                    dve.scalar_tensor_tensor(out=kl[0:D, c * 512:(c + 1) * 512], in0=ps_a[0:D, c % 2, :],
                                             scalar=bk2[0:D, :], in1=kh[0:D, c * 512:(c + 1) * 512].bitcast(F32),
                                             op0=ALU.add, op1=ALU.subtract).then_inc(kl_ready, 1)
                low_q(b, 0, 0)
                new_live(b, 0, 0)
                for a in range(QT * KC):
                    reduce_a(b, 0, a)
                whole_max(b, 0)
                take_max(b, 0, 0)
                low_q(b, 1, 1)
                new_live(b, 1, 1)

            def reduce_a(b, g, a):
                dve.wait_ge(a_full, (b * G + g) * (QT * KC) + a + 1)
                dve.tensor_reduce(mx[:, a // KC, a % KC:a % KC + 1], ps_a[:, a % 2, :], AX.X, ALU.max).then_inc(a_used, 1)

            def whole_max(b, g):
                dve.wait_ge(a_used, (b * G + g + 1) * (QT * KC))
                dve.tensor_reduce(rowmax[:], mx[:], AX.X, ALU.max).then_inc(max_ready, 1)

            def take_max(b, g, par):
                dve.wait_ge(mrow_full, b * G + g + 1)
                dve.scalar_tensor_tensor(
                    out=q2[D:D + QT, par, :].rearrange("p (q c) -> p q c", q=QT),
                    in0=ps_m[D:D + QT, 0:P].unsqueeze(1).to_broadcast([QT, QT, P]), scalar=LIFT,
                    in1=own[D:D + QT, :, :], op0=ALU.subtract, op1=ALU.mult).then_inc(mrow_ready, 1)

            def group(b, g, par, last):
                order = Order(dve, s_dve2, (b * G + g) * ND2)
                if not last:
                    for a in range(QT * KC):
                        reduce_a(b, g + 1, a)
                    whole_max(b, g + 1)
                    take_max(b, g + 1, 1 - par)
                mine = h[:, bass.ds(b % 2 * N + g * QT, QT), :]
                more = has_query_product(g)
                if more:
                    low_q(b, g + 2, par)
                dve.wait_ge(oT_ready, b * G + g + 1)
                dve.tensor_copy(oT[D:D + 1, :], live[D:D + 1, par, :]).then_inc(live_in, 1)
                if more:
                    dve.wait_ge(live_in, b * G + g + 1)
                    new_live(b, g + 2, par)
                dve.wait_ge(post_full, b * G + g + 1)
                got_o = ps_m[:, 0:QT * (D + 2)].rearrange("p (q d) -> p q d", d=D + 2)
                order.then(dve.reciprocal(post[:, 0, :], got_o[:, :, D:D + 1].rearrange("p q a -> p (q a)")))
                order.then(dve.tensor_tensor(post[:, 1, :], post[:, 0, :],
                                             got_o[:, :, D + 1:D + 2].rearrange("p q a -> p (q a)"), ALU.mult))
                order.then(dve.tensor_tensor(att[:], got_o[:, :, 0:D],
                                             post[:, 1, :].unsqueeze(2).to_broadcast([P, QT, D]), ALU.mult))
                order.then(dve.tensor_tensor(att[:], att[:], bo_all[:].unsqueeze(1).to_broadcast([P, QT, D]), ALU.add))
                dve.tensor_tensor(mine, mine, att[:], ALU.add).then_inc(h_ready, 1)
                assert order.n == ND2

            def low_q(b, g, par):
                dve.wait_ge(qh_ready, b * G + g + 1)
                dve.scalar_tensor_tensor(out=q1[D:P, par, :], in0=ps_m[D:P, :], scalar=bq2[D:P, :],
                                         in1=q1[D:P, par, :].bitcast(F32), op0=ALU.add, op1=ALU.subtract)
                dve.tensor_scalar(live_q[D:D + 1, :], ps_m[D:D + 1, :], bq2[D:D + 1, :], 0.0,
                                  ALU.add, ALU.not_equal).then_inc(q_ready, 1)

            def new_live(b, g, par):
                dve.wait_ge(q_ready, b * G + g + 1)
                dve.scalar_tensor_tensor(out=live[D:D + 1, par, :], in0=kh[D:D + 1, bass.ds(g * GQ, GQ)].bitcast(F32), scalar=0.0,
                                         in1=live_q[D:D + 1, :], op0=ALU.not_equal, op1=ALU.mult)

            def finish(b):
                order = Order(dve, s_dve3, b * ND3)
                wait_apart(dve, h_ready, G * (b + 1))
                wait_apart(dve, xn_free, b + 1)
                layer_norm(order, h[:, bass.ds(b % 2 * N, N), :], xw[:, :, 0:D], b, 1)
                wts = xw[:, :, D:D + 1].rearrange("p n a -> p (n a)")
                numbers = xw[:, :, D + 1:D + 2].rearrange("p n a -> p (n a)")

                def over_e(v):
                    return v.unsqueeze(2).to_broadcast([P, N, E])

                def over_n(v):
                    return v.unsqueeze(1).to_broadcast([P, N, E])

                dve.wait_ge(lg_full, b + 1)
                order.then(dve.tensor_reduce(lg[:], ps_m[:].rearrange("p (n t e) -> p n e t", e=E, t=2), AX.X, ALU.add))
                order.then(dve.tensor_tensor(lg[:], lg[:], over_n(gb_all[:]), ALU.add))
                order.then(dve.tensor_reduce(rt[:, 0, :], lg[:], AX.X, ALU.max))
                order.then(dve.tensor_tensor(oneh[:], lg[:], over_e(rt[:, 0, :]), ALU.is_equal))
                order.then(dve.tensor_tensor(oneh[:], oneh[:], over_n(e_down[:]), ALU.mult))
                order.then(dve.tensor_reduce(rt[:, 1, :], oneh[:], AX.X, ALU.max))
                order.did(dve.tensor_tensor(oneh[:], oneh[:], over_e(rt[:, 1, :]), ALU.is_equal))
                dve.tensor_tensor(lg[:], lg[:], over_e(rt[:, 0, :]), ALU.subtract).then_inc(lg_centred, 1)
                dve.wait_ge(lg_exp, b + 1)
                order.then(dve.tensor_reduce(rt[:, 2, :], cum[:, 0, :, :], AX.X, ALU.add))
                order.did(dve.reciprocal(rt[:, 3, :], rt[:, 2, :]))
                order.then(dve.tensor_copy(cum[:, 0, :, :], oneh[:]))
                src = 0
                for s in (1, 2, 4, 8, 16):
                    order.did(dve.tensor_copy(cum[:, 1 - src, 0:s, :], cum[:, src, 0:s, :]))
                    ins = dve.tensor_tensor(cum[:, 1 - src, s:N, :], cum[:, src, s:N, :], cum[:, src, 0:N - s, :], ALU.add)
                    src = 1 - src
                    if s < 16:
                        order.then(ins)
                    else:
                        ins.then_inc(cp_ready, 1)
                dve.wait_ge(cb_full, b + 1)
                order.did(dve.tensor_tensor(carry[:], carry[:], cum[:, 1, N - 1, :], ALU.add))
                order.then(dve.tensor_copy(cbase[:], ps_a[:, 0, 0:E]))
                order.then(dve.tensor_tensor(cum[:, 0, :, :], cum[:, 1, :, :], over_n(cbase[:]), ALU.add))
                order.then(dve.tensor_tensor(cum[:, 0, :, :], cum[:, 0, :, :], oneh[:], ALU.mult))
                order.did(dve.tensor_reduce(rt[:, 4, :], cum[:, 0, :, :], AX.X, ALU.add))
                order.then(dve.tensor_tensor(oneh[:], oneh[:], over_n(e_base[:]), ALU.mult))
                order.then(dve.tensor_reduce(rt[:, 5, :], oneh[:], AX.X, ALU.add))
                order.then(dve.tensor_scalar(rt[:, 0, :], rt[:, 4, :], float(CAP), None, ALU.is_le))
                order.did(dve.tensor_tensor(wts, rt[:, 3, :], rt[:, 0, :], ALU.mult))
                order.did(dve.tensor_scalar(rt[:, 1, :], rt[:, 0, :], -4.0 * E * CAP, 4.0 * E * CAP, ALU.mult, ALU.add))
                order.did(dve.tensor_copy(numbers, token[:]))
                order.then(dve.tensor_scalar(rt[:, 2, :], rt[:, 4, :], -1.0, None, ALU.add))
                order.then(dve.tensor_tensor(rt[:, 2, :], rt[:, 2, :], rt[:, 5, :], ALU.add))
                order.did(dve.tensor_scalar(token[:], token[:], float(S), None, ALU.add))
                dve.tensor_tensor(put_at[:], rt[:, 2, :], rt[:, 1, :], ALU.add).then_inc(put_ready, 1)
                assert order.n == ND3, order.n

            images(dve, prepare, group, finish)

            with dve.Fori(0, E // 2) as pair:
                order = Order(dve, s_dve4, pair * ND4)

                def parts(c):
                    k = pair * (2 * CH) + c
                    wait_apart(dve, xm_in[c % XR], (pair * 2 + c // XR + 1) * 16)
                    if c >= 1:
                        wait_apart(dve, xmT_full, k)
                    order.then(dve.tensor_copy(xmhl[:, :, 0, :].bitcast(F32R), xm[:, c % XR, :, 0:D]))
                    dve.tensor_tensor(xmhl[:, :, 1, :].bitcast(F32R), xm[:, c % XR, :, 0:D], xmhl[:, :, 0, :],
                                      ALU.subtract).then_inc(xmhl_ready, 1)

                def to_add(c):
                    k = pair * (2 * CH) + c
                    rows = ym[:, c % 2, :, :]
                    if c >= 2:
                        dve.wait_ge(y_out[c % 2], (pair * CH + c // 2) * 64)
                    dve.wait_ge(ym_full, k + 1)
                    dve.tensor_copy(add_at[:, c % 2, :], xm[:, c % XR, :, D + 1:D + 2].rearrange("p a b -> p (a b)"))
                    dve.tensor_tensor(rows, ps_m[:, 0:4 * D].rearrange("p (a d) -> p a d", d=D),
                                      xm[:, c % XR, :, D:D + 1].to_broadcast([P, 4, D]), ALU.mult).then_inc(ym_read, 1)
                    dve.wait_ge(ym_read, k + 1 + XR)
                    order.then(dve.tensor_scalar(yscr, rows, 0.0, None, ALU.min))
                    order.then(dve.scalar_tensor_tensor(out=rows, in0=rows, scalar=0.0, in1=yscr, op0=ALU.max, op1=ALU.add))
                    order.did(dve.tensor_scalar(yscr, rows, 1e4, -1e4, ALU.min, ALU.max))
                    last = order.did(dve.tensor_scalar(bad, rows, 0.0, 0.0, ALU.mult, ALU.not_equal))
                    wait_apart(dve, s_dve4, order.base + last)
                    dve.copy_predicated(out=rows, mask=bad, data=yscr).then_inc(ym_ready, 1)

                parts(0)
                for c in range(2 * CH):
                    k = pair * (2 * CH) + c
                    e = pair * 2 + c // CH
                    if c % CH == 0:
                        dve.wait_ge(w_in, (e + 1) * 48)
                        order.then(dve.tensor_copy(w1p[:, c // CH, 0, :], w1s[:]))
                        order.then(dve.tensor_tensor(w1p[:, c // CH, 1, :], w1s[:], w1p[:, c // CH, 0, :].bitcast(F32), ALU.subtract))
                        dve.sem_inc(w_free, 1)
                        dve.sem_inc(w_ready, 1)
                    dve.wait_ge(hid_full, (k + 1) * 2)
                    dve.tensor_scalar(hid[:, c % 2, 1, :], ps_s[:, 2 * (c % 2) + 1, :],
                                      b1c[:, bass.ds(e, 1), 1:2].rearrange("p a b -> p (a b)"), 0.0,
                                      ALU.add, ALU.max).then_inc(hid_b, 1)
                    if c + 1 < 2 * CH:
                        parts(c + 1)
                    if c >= 1:
                        to_add(c - 1)
                    dve.wait_ge(yT_full, k + 1)
                    dve.tensor_scalar(yT[c % 2], ps_o[0:D, :], b2c[:, bass.ds(e, 1)], None, ALU.add).then_inc(yT_ready, 1)
                to_add(2 * CH - 1)
                assert order.n == ND4, order.n
                dve.wait_ge(y_out[0], (pair + 1) * (64 * CH))
                dve.wait_ge(y_out[1], (pair + 1) * (64 * CH))


_INS = ['x', 'L0_tok_conv1_w', 'L0_tok_conv1_b', 'L0_tok_bn_gamma', 'L0_tok_bn_beta', 'L0_tok_bn_mean',
        'L0_tok_bn_var', 'L0_tok_conv2_w', 'L0_tok_conv2_b', 'L0_attn_Wq', 'L0_attn_bq', 'L0_attn_Wk', 'L0_attn_bk',
        'L0_attn_Wv', 'L0_attn_bv', 'L0_attn_Wo', 'L0_attn_bo', 'L0_ffn_gate_w', 'L0_ffn_gate_b', 'L0_ffn_w1',
        'L0_ffn_b1', 'L0_ffn_w2', 'L0_ffn_b2']


def kernel(**inputs):
    import concourse.bacc as _bacc
    from concourse.bass_utils import run_bass_kernel_spmd as _run

    nc = _bacc.Bacc("TRN2", target_bir_lowering=False, num_devices=1)
    arrays, args = {}, []
    for name in _INS:
        a = np.ascontiguousarray(inputs[name])
        arrays[f"in_{name}"] = a
        args.append(nc.dram_tensor(f"in_{name}", a.shape, mybir.dt.from_np(a.dtype), kind="ExternalInput").ap())
    b, c, hh, ww = inputs['x'].shape
    slots = -(-5 * b * c * hh // 4)
    args.append(nc.dram_tensor("out_0", (b, c * hh, ww), F32, kind="ExternalOutput").ap())
    args.append(nc.dram_tensor("slots_x", (slots, ww + 2), F32).ap())
    tower(nc, *args)
    r = _run(nc, [arrays], core_ids=[0])
    return r.results[0]["out_0"]
```

```python
from contextlib import ExitStack

import numpy as np
import concourse.bass as bass
from concourse import mybir

F32 = mybir.dt.float32
F32R = mybir.dt.float32r
F16 = mybir.dt.float16
I32 = mybir.dt.int32
ALU = mybir.AluOpType
ACT = mybir.ActivationFunctionType
AX = mybir.AxisListType

P = 128
LN_EPS = 1e-5
BN_EPS = 1e-5


class Order:

    def __init__(self, eng, sem, base):
        self.eng, self.sem, self.base, self.n = eng, sem, base, 0

    def did(self, ins):
        ins.then_inc(self.sem, 1)
        self.n += 1
        return self.n

    def need(self, n):
        self.eng.wait_ge(self.sem, self.base + n)

    def then(self, ins):
        self.need(self.did(ins))


def tower(nc, x, conv1_w, conv1_b, bn_gamma, bn_beta, bn_mean, bn_var, conv2_w, conv2_b,
          Wq, bq, Wk, bk, Wv, bv, Wo, bo, gate_w, gate_b, w1, b1, w2, b2, out, slots_x):
    B, C, HH, WW = x.shape
    CR = conv1_w.shape[0]
    TAPS = conv2_w.shape[0]
    D = WW
    S = C * HH
    N = S // P
    RH = HH // 2
    E = gate_w.shape[1]
    F = w1.shape[2]
    CAP = -(-5 * B * S // (4 * E))
    GQ = 512
    G = S // GQ
    QT = GQ // P
    KC = S // 512
    STEPS = N // 2
    SCALE = float(D) ** -0.5
    LIFT = 8.0 * float(np.log(2.0)) / SCALE
    assert (B, C, HH, WW, CR, TAPS, E, F) == (4, 64, 64, 64, 16, 9, 8, 256)
    HALF = RH * WW
    PCH = HALF // 512
    FC = F // P
    CH = CAP // 512
    assert CH * 512 == CAP
    CENTER_FIRST = [4, 0, 1, 2, 3, 5, 6, 7, 8]
    FR = 20
    NOBODY = float(2 ** 20)
    LAG = 3
    PLAIN = ["", "", "", "aaa", "aaa", "aa", "a", "aaa", "aaa", "aaa", "aaa", "aaa", "aaa", "aaa", "aa", "", ""]
    RING = {
        "plain": PLAIN, "last": [""] * 17,
        "norm": ["", "", "", "", "aaa", "aa", "aaa", "aaaa", "aaaa", "aaaa", "", "aaaa", "aaaa", "", "aaaa", "", ""],
        "root": ["", "", "", "aaaa", "aaaa", "a", "a", "aaaa", "aaaa", "", "aa", "", "aaaa", "aaaa", "aaaa", "", ""],
        "taps": ["", "", "tt", "tt", "ttaa", "aaaa", "", "taa", "aaaa", "taa", "aaaa", "taaa", "aaaa", "aaa", "aaaa", "", ""],
        "keys": ["", "", "k", "a", "aak", "a", "a", "aaa", "k", "aaak", "aaak", "aaaa", "aak", "aaa", "ka", "aaak", "aaaaa"],
        "logits": ["", "", "", "", "aaal", "aaal", "aaal", "aaal", "aaaal", "aaaal", "aaaal", "aaaal", "aaaa", "", "", "", "c"],
    }
    BANK = {
        "plain": {0: "q", 5: "post"},
        "last": {5: "post"},
        "taps": {-1: "conv", 1: "q", 6: "post"},
        "keys": {-1: "T0", 1: "q", 3: "T1", 5: "post", 7: "T2", 8: "T3", 9: "T4", 10: "T5", 11: "T6", 12: "T7"},
        "logits": {0: "post", 1: "q", 3: "T0", 4: "T1", 5: "T2", 6: "T3", 7: "T4", 8: "T5", 9: "T6", 10: "T7"},
    }
    RP = 4
    R32 = 4
    XR = CH
    EARLY = 24
    CHOOSE = 13
    BANK["norm"] = BANK["root"] = BANK["plain"]

    with ExitStack() as ctx:
        ctx.enter_context(nc.allow_non_contiguous_dma(reason="small weights, loaded once"))
        def sb(name, shape, dt=F32):
            return ctx.enter_context(nc.sbuf_tensor(name, shape, dt))

        def psum(name, shape):
            return ctx.enter_context(nc.psum_tensor(name, shape, F32))

        def sem(name):
            return ctx.enter_context(nc.semaphore(name))

        out_rows = out.rearrange("b s d -> (b s) d")

        ps_s = psum("ps_s", [P, 4, 512])
        ps_a = psum("ps_a", [P, 2, 512])
        ps_o = psum("ps_o", [P, 512])
        ps_m = psum("ps_m", [P, 512])

        ident = sb("ident", [P, P])
        before = sb("before", [P, P])
        ones = sb("ones", [P, P])
        wq_t = sb("wq_t", [P, 2, D])
        wk_t = sb("wk_t", [P, 2, D])
        wq_p = sb("wq_p", [P, 2, P], F32R)
        wk_p = sb("wk_p", [P, 2, P], F32R)
        woT = sb("woT", [D, D])
        wvx = sb("wvx", [D, P])
        wg = sb("wg", [P, D + 2])
        bq2 = sb("bq2", [P, 1])
        bk2 = sb("bk2", [P, 1])
        bo_all = sb("bo_all", [P, D])
        w1bd = sb("w1bd", [P, P])
        bn_raw = sb("bn_raw", [P, 5])
        bn_t = sb("bn_t", [P, 4])
        bn_scale = sb("bn_scale", [P, 1])
        bn_bias = sb("bn_bias", [P, 1])
        cw2 = sb("cw2", [P, TAPS])
        tapw = sb("tapw", [P, 2, TAPS, C, 2], F32R)
        gw = sb("gw", [P, E])
        gw_p = sb("gw_p", [P, 2, E], F32R)
        gb_all = sb("gb_all", [P, E])
        e_down = sb("e_down", [P, E])
        e_base = sb("e_base", [P, E])
        b1c = sb("b1c", [P, E, FC])
        b2c = sb("b2c", [D, E])

        xh = sb("xh", [P, RH + 2, WW])
        xc = sb("xc", [P, HALF])
        y = sb("y", [P, 2, 512], F32R)
        y32 = sb("y32", [P, 512])
        tmp = sb("tmp", [P, 2, 8, WW])
        h = sb("h", [P, 2 * N, D])
        xcen = sb("xcen", [P, N, D])
        xhl = sb("xhl", [P, N, 2, D])
        fill = xcen[:].rearrange("p n d -> p (n d)")[:, 0:FR * (D + 2)].rearrange("p (a d) -> p a d", a=FR)
        ln_s = sb("ln_s", [P, 2, 3, N])
        ln_q = sb("ln_q", [P, 2, N])
        var = sb("var", [P, 2 * N])
        sd = sb("sd", [P, 2 * N])
        xs = sb("xs", [P, N, P], F16)
        xT = sb("xT", [P, S], F32R)
        kh = sb("kh", [P, S], F32R)
        kl = sb("kl", [P, S], F32R)
        q1 = sb("q1", [P, 2, GQ], F32R)
        q2 = sb("q2", [P, 2, GQ], F32R)
        own = sb("own", [D + QT, QT, P])
        live_q = sb("live_q", [65, GQ])
        live = sb("live", [65, 2, GQ])
        mx = sb("mx", [P, QT, KC])
        rowmax = sb("rowmax", [P, QT])
        p32 = sb("p32", [P, R32, 1024])
        ph = sb("ph", [P, RP, 1024], F16)
        pl = sb("pl", [P, RP, 1024], F16)
        oT = sb("oT", [P, GQ])
        post = sb("post", [P, 2, QT])
        att = sb("att", [P, QT, D])

        lg = sb("lg", [P, N, E])
        lg_e = att[:].rearrange("p a d -> p (a d)").rearrange("p (n e) -> p n e", n=N)
        rt = sb("rt", [P, 6, N])
        oneh = sb("oneh", [P, N, E])
        cum = sb("cum", [P, 2, N, E])
        carry = sb("carry", [P, E])
        cbase = sb("cbase", [P, E])
        xw = sb("xw", [P, N, D + 2])
        token = sb("token", [P, N])
        put_at = sb("put_at", [P, N], I32)
        put_now = sb("put_now", [P, EARLY // 4], I32)
        xw_now = sb("xw_now", [P, EARLY // 4, D + 2])

        add_at = sb("add_at", [P, XR, 4], I32)
        w_nat = p32[0:D, 2, 0:8 * D].rearrange("p (w t d) -> p w t d", w=4, t=2)
        xm = xcen[:].rearrange("p n d -> p (n d)")[:, 0:XR * 4 * (D + 2)].rearrange("p (c a d) -> p c a d", c=XR, a=4)
        p32_rest = p32[:, 2:4, :].rearrange("p c w -> p (c w)")
        xmhl = p32_rest[:, 0:8 * D].rearrange("p (a t d) -> p a t d", a=4, t=2)
        ym = p32_rest[:, 8 * D:(8 + 4 * XR) * D].rearrange("p (c a d) -> p c a d", c=XR, a=4)
        yscr = att[:]
        xs32 = xs[:].rearrange("p n d -> p (n d)").bitcast(F32)
        w1s = xs32[:, 0:F]
        w2s = xs32[:, F:F + 2 * FC * D].rearrange("p (t f d) -> p t f d", t=2, f=FC)
        w1p = kl[:, 0:4 * F].rearrange("p (e t f) -> p e t f", e=2, t=2)
        bad = lg[:].rearrange("p (a n) e -> p a (n e)", a=4).bitcast(I32)
        xmT = xT[:, 0:1024].rearrange("p (c s) -> p c s", c=2)
        yT = (oT[0:D, :], y32[0:D, :])
        hid = p32[:, 0:2, :].rearrange("p c (f s) -> p c f s", f=FC)

        consts_in = sem("consts_in")
        zero_out = sem("zero_out")
        made = sem("made")
        cleared = sem("cleared")
        s_dset = sem("s_dset")
        s_pset = sem("s_pset")
        s_aset = sem("s_aset")
        x_in = sem("x_in")
        x_free = sem("x_free")
        conv1 = sem("conv1")
        y_high = sem("y_high")
        y_ready = sem("y_ready")
        s_tap = sem("s_tap")
        s_ln1 = sem("s_ln1")
        s_ln2 = sem("s_ln2")
        s_cast = sem("s_cast")
        var_ready = sem("var_ready")
        sd_ready = sem("sd_ready")
        xn_ready = sem("xn_ready")
        xt_full = sem("xt_full")
        xt_ready = sem("xt_ready")
        kh_ready = sem("kh_ready")
        xs_ready = sem("xs_ready")
        x2_split = sem("x2_split")
        x2_full = sem("x2_full")
        x2_ready = sem("x2_ready")
        h_free = sem("h_free")
        q_full = sem("q_full")
        qh_ready = sem("qh_ready")
        q_ready = sem("q_ready")
        a_full = sem("a_full")
        a_used = sem("a_used")
        max_ready = sem("max_ready")
        mrow_full = sem("mrow_full")
        mrow_ready = sem("mrow_ready")
        s_full = sem("s_full")
        ph_ready = sem("ph_ready")
        pl_ready = sem("pl_ready")
        av_done = sem("av_done")
        oT_ready = sem("oT_ready")
        live_ready = sem("live_ready")
        live_in = sem("live_in")
        post_full = sem("post_full")
        s_dve2 = sem("s_dve2")
        h_ready = sem("h_ready")
        lg_centred = sem("lg_centred")
        lg_exp = sem("lg_exp")
        s_dve3 = sem("s_dve3")
        cp_ready = sem("cp_ready")
        put_ready = sem("put_ready")
        now_ready = sem("now_ready")
        put_done = sem("put_done")
        put_late = sem("put_late")
        w_in = sem("w_in")
        w_free = sem("w_free")
        w_ready = sem("w_ready")
        xm_in = [sem(f"xm_in{i}") for i in range(XR)]
        xmT_full = sem("xmT_full")
        xmhl_ready = sem("xmhl_ready")
        xmT_ready = sem("xmT_ready")
        hid_full = sem("hid_full")
        hid_a = sem("hid_a")
        hid_b = sem("hid_b")
        yT_full = sem("yT_full")
        yT_ready = sem("yT_ready")
        ym_full = sem("ym_full")
        ym_read = sem("ym_read")
        ym_ready = sem("ym_ready")
        y_out = [sem(f"y_out{i}") for i in range(XR)]
        ym_free = sem("ym_free")
        s_dve4 = sem("s_dve4")
        stored = sem("stored")
        waits = {e.engine: sem(f"waits_{n}") for n, e in (("pe", nc.tensor), ("act", nc.scalar),
                                                          ("dve", nc.vector), ("pool", nc.gpsimd),
                                                          ("sp", nc.sync))}

        def wait_apart(eng, semaphore, value):
            eng.wait_ge(semaphore, value)
            eng.sem_inc(waits[eng.engine], 1)

        TAP_ENTRIES = PCH * TAPS
        KEY_ENTRIES = KC + QT * KC
        START = TAP_ENTRIES + KEY_ENTRIES
        START_K = [TAP_ENTRIES + (0 if c == 0 else 1 + (c - 1) * (QT + 1)) for c in range(KC)]
        START_A = [TAP_ENTRIES + min(2 + c * (QT + 1), KEY_ENTRIES - QT) for c in range(KC)]
        count = {kind: len("".join(RING[kind])) for kind in RING}
        ROUND = 4 * count["taps"] + count["norm"] + count["root"] + count["keys"] + count["logits"]
        assert count["plain"] == KC * QT and count["taps"] == KC * QT + TAPS
        assert count["keys"] == KEY_ENTRIES and count["logits"] == KC * QT + KC + 1

        def stream(eng, start, group, finish):
            start()
            group(0, 0, 0, "plain", START, True)
            with eng.Fori(0, B - 1) as b:
                base = START + count["plain"] + b * ROUND
                with eng.Fori(0, 2) as pair:
                    for i in range(2):
                        group(b, pair * 2 + i + 1, 1 - i, "taps",
                              base + pair * (2 * count["taps"]) + i * count["taps"], True)
                base = base + 4 * count["taps"]
                group(b, 5, 1, "norm", base, True)
                base = base + count["norm"]
                group(b, 6, 0, "root", base, True)
                base = base + count["root"]
                group(b, 7, 1, "keys", base, True)
                base = base + count["keys"]
                group(b + 1, 0, 0, "logits", base, True)
            base = START + count["plain"] + (B - 1) * ROUND
            with eng.Fori(0, 2) as pair:
                for i in range(2):
                    group(B - 1, pair * 2 + i + 1, 1 - i, "plain",
                          pair * (2 * count["plain"]) + (base + i * count["plain"]), False)
            group(B - 1, 5, 1, "norm", base + 4 * count["plain"], False)
            group(B - 1, 6, 0, "root", base + 5 * count["plain"], False)
            group(B - 1, 7, 1, "last", base + 6 * count["plain"], False)
            finish(base + 6 * count["plain"])

        def entries(kind, j):
            before_j = "".join(RING[kind][:j])
            for i, what in enumerate(RING[kind][j]):
                seen = before_j + RING[kind][j][:i]
                yield len(seen), what, seen.count(what)

        FILLS = E * CAP // (FR * P)
        N_CONST = 10 + 4 * 8 + 2 + 5
        ND1 = TAPS
        ND2 = 4
        ND3 = 31
        ND4 = 2 * 2 + 2 * CH * 5
        ROUNDS = B + 1

        block = ctx.enter_context(nc.Block())

        @block.sync
        def _(sp):
            for i, w in enumerate((Wq, Wk, Wv, Wo)):
                for t in range(2 if i < 2 else 1):
                    sp.dma_start(w_nat[:, i, t, :], w).then_inc(consts_in, 16)
            for dst, v in ((bq2, bq), (bk2, bk)):
                for half in range(2):
                    sp.dma_start(dst[D * half:D * (half + 1), :], v.rearrange("(a b) -> a b", b=1)).then_inc(consts_in, 16)
            sp.wait_ge(made, 4)
            for low in range(2):
                for half in range(2):
                    row = 64 * low + 32 * half
                    sp.dma_start(w1bd[C * half:C * (half + 1), row:row + CR],
                                 conv1_w.rearrange("o c -> c o")).then_inc(consts_in, 16)
                    for i, v in enumerate((conv1_b, bn_gamma, bn_beta, bn_mean, bn_var)):
                        sp.dma_start(bn_raw[row:row + CR, i:i + 1],
                                     v.rearrange("(a b) -> a b", b=1)).then_inc(consts_in, 16)
                    sp.dma_start(cw2[row:row + CR, :], conv2_w.rearrange("k o -> o k")).then_inc(consts_in, 16)
                    sp.dma_start(cw2[row + CR:row + CR + 1, :],
                                 conv2_b.rearrange("(b a) -> b a", b=1)).then_inc(consts_in, 16)
                sp.dma_start(gw[D * low:D * (low + 1), :], gate_w).then_inc(consts_in, 16)
            sp.dma_start(wvx[:, 63:64], bv.rearrange("(a b) -> a b", b=1)).then_inc(consts_in, 16)
            sp.dma_start(bo_all[:], bo.partition_broadcast(P)).then_inc(consts_in, 16)
            sp.dma_start(gb_all[:], gate_b.partition_broadcast(P)).then_inc(consts_in, 16)
            sp.dma_start(b1c[:], b1.rearrange("e (f p) -> p e f", p=P)).then_inc(consts_in, 16)
            sp.dma_start(b2c[:], b2.rearrange("e d -> d e")).then_inc(consts_in, 16)

            sp.wait_ge(cleared, 1)

            def load_x(b):
                for half in range(2):
                    lo = 0 if half == 0 else RH - 1
                    sp.dma_start(
                        xh[half:P:2, 1 - half:RH + 2 - half, :],
                        x[bass.ds(b, 1), :, lo:lo + RH + 1, :].rearrange("a c r w -> (a c) r w")).then_inc(x_in, 16)
                    sp.dma_start(
                        xc[C * half:C * (half + 1), :],
                        x[bass.ds(b, 1), :, RH * half:RH * (half + 1), :].rearrange("a c r w -> (a c) (r w)"),
                    ).then_inc(x_in, 16)

            def store_h(b):
                wait_apart(sp, h_ready, G * (b + 1))
                sp.dma_start(out[bass.ds(b, 1)].rearrange("a (p n) d -> p (a n) d", p=P),
                             h[:, bass.ds(b % 2 * N, N), :]).then_inc(stored, 16)
                wait_apart(sp, stored, (b + 1) * 16)
                sp.sem_inc(h_free, 1)

            load_x(0)
            sp.wait_ge(x_free, PCH)
            load_x(1)
            with sp.Fori(0, B - 2) as b:
                wait_apart(sp, x_free, PCH * (b + 2))
                load_x(b + 2)
                store_h(b)
            store_h(B - 2)
            store_h(B - 1)

            with sp.Fori(0, E // 2) as pair:
                for par in range(2):
                    sp.wait_ge(w_free, pair * 2 + par + 1)
                    e = pair * 2 + par
                    for low in range(2):
                        sp.dma_start(w1s[D * low:D * (low + 1), :],
                                     w1[bass.ds(e, 1)].rearrange("a d f -> (a d) f")).then_inc(w_in, 16)
                    sp.dma_start(w2s[:, par, :, :],
                                 w2[bass.ds(e, 1)].rearrange("a (f p) d -> p (a f) d", p=P)).then_inc(w_in, 16)
                    for a in range(CH):
                        c = par * CH + a
                        k = pair * (2 * CH) + c
                        if c < XR:
                            sp.wait_ge(put_done, 16 * EARLY * ROUNDS)
                            sp.wait_ge(put_late, 16 * (N - EARLY) * ROUNDS)
                        sp.wait_ge(ym_read, k + 1)
                        sp.dma_start(xm[:, c % XR, :, :],
                                     slots_x[bass.ds(k * 512, 512), :].rearrange("(p a) d -> p a d", p=P),
                                     ).then_inc(xm_in[c % XR], 16)
            sp.wait_ge(stored, 16 * B)
            sp.wait_ge(zero_out, 16 * FILLS)

        @block.gpsimd
        def _(pool):
            pool.memset(bn_raw[:], 0.0).then_inc(made, 1)
            pool.memset(w1bd[:], 0.0).then_inc(made, 1)
            pool.memset(wvx[:], 0.0).then_inc(made, 1)
            pool.memset(cw2[:], 0.0).then_inc(made, 1)
            pool.memset(ones[:], 1.0).then_inc(made, 1)
            pool.memset(fill[:, :, 0:D + 1], 0.0)
            pool.memset(fill[:, :, D + 1:D + 2], NOBODY).then_inc(made, 1)
            pool.wait_ge(made, 6)
            pool.affine_select(out=ident[:], in_=ones[:], compare_op=ALU.is_equal, fill=0.0, base=0,
                               pattern=[[1, P]], channel_multiplier=-1).then_inc(made, 1)
            pool.affine_select(out=before[:], in_=ones[:], compare_op=ALU.is_gt, fill=0.0, base=0,
                               pattern=[[1, P]], channel_multiplier=-1).then_inc(made, 1)
            pool.iota(token[:], pattern=[[1, N]], base=0, channel_multiplier=N,
                      allow_small_or_imprecise_dtypes=True).then_inc(made, 1)
            pool.iota(e_down[:], pattern=[[-1, E]], base=E, channel_multiplier=0,
                      allow_small_or_imprecise_dtypes=True).then_inc(made, 1)
            pool.iota(e_base[:], pattern=[[CAP, E]], base=0, channel_multiplier=0,
                      allow_small_or_imprecise_dtypes=True).then_inc(made, 1)

            pool.memset(xw[:], 0.0)
            pool.memset(put_at[:], 4 * E * CAP).then_inc(made, 1)
            pool.wait_ge(made, 12)
            pool.sem_inc(put_ready, 1)
            pool.wait_ge(zero_out, 16 * FILLS)

            def put(at, rows, done):
                pool.indirect_dma_start(slots_x, bass.IndirectOffsetOnAxis(ap=at, axis=0),
                                        rows, None, bounds_check=E * CAP - 1,
                                        oob_is_err=False).then_inc(done, 16)

            PUT_AT = (2, 4, 6, 8, 10, 12)
            LATE_AT = (1, 2, 4, 6, 8, 10, 12, 14)

            def group(im, g, par, kind, base, more):
                t0 = (im * G + g) * STEPS
                for j in range(STEPS):
                    pool.wait_ge(ph_ready, t0 + j + 1)
                    pool.tensor_tensor(out=pl[:, j % RP, :], in0=p32[:, j % R32, :], in1=ph[:, j % RP, :],
                                       op=ALU.subtract).then_inc(pl_ready, 1)
                    if kind == "taps" or (kind == "plain" and not more):
                        if j == 0:
                            wait_apart(pool, put_ready, im + 1)
                            pool.tensor_copy(xw_now[:], xw[:, bass.ds((g - 1) * (EARLY // 4), EARLY // 4), :])
                            pool.tensor_copy(put_now[:], put_at[:, bass.ds((g - 1) * (EARLY // 4), EARLY // 4)]).then_inc(now_ready, 1)
                            wait_apart(pool, now_ready, im * 4 + g)
                        if j in PUT_AT:
                            n = PUT_AT.index(j)
                            put(put_now[:, n:n + 1], xw_now[:, n, :], put_done)
                        if j == STEPS - 1:
                            pool.wait_ge(put_done, (im * 4 + g) * (4 * EARLY))
                    if kind == "norm" and j in LATE_AT:
                        n = EARLY + LATE_AT.index(j)
                        put(put_at[:, n:n + 1], xw[:, n, :], put_late)

            def finish(base):
                wait_apart(pool, put_ready, B + 1)
                for n in range(N):
                    put(put_at[:, n:n + 1], xw[:, n, :], put_done if n < EARLY else put_late)

            stream(pool, lambda: None, group, finish)

            pool.wait_ge(stored, 16 * B)
            with pool.Fori(0, E // 2) as pair:
                for c in range(2 * CH):
                    k = pair * (2 * CH) + c
                    wait_apart(pool, ym_ready, k + 1)
                    for a in range(4):
                        pool.indirect_dma_start(out_rows, bass.IndirectOffsetOnAxis(ap=add_at[:, c % XR, a:a + 1], axis=0),
                                                ym[:, c % XR, a, :], None, bounds_check=B * S - 1, oob_is_err=False,
                                                compute_op=ALU.add).then_inc(y_out[c % XR], 16)
                    for done in ([c - 1] if c >= 1 else []) + ([c] if c == 2 * CH - 1 else []):
                        pool.wait_ge(y_out[done % XR], (pair * 2 + done // XR + 1) * 64)
                        pool.sem_inc(ym_free, 1)
            for a in range(XR):
                pool.wait_ge(y_out[a], 64 * E * CH // XR)

        @block.tensor
        def _(pe):
            pe.wait_ge(made, 8)
            pe.wait_ge(consts_in, 16 * N_CONST)
            for i in range(2):
                pe.transpose(ps_m[:, D * i:D * (i + 1)], w_nat[:, i, :, :].rearrange("o t w -> o (t w)"), ident[0:D, 0:D])
            pe.transpose(ps_m[0:D, 2 * D:3 * D], w_nat[:, 3, 0, :], ident[0:D, 0:D]).then_inc(s_pset, 1)
            pe.wait_ge(s_dset, 1)
            pe.matmul(ps_m[:, 256:256 + D], wvx[:], woT[:], start=True, stop=True).then_inc(s_pset, 1)

            def q_product(t, g):
                for part in range(2):
                    mm = pe.matmul(ps_m[:], wq_p[:, part, :], xT[:, bass.ds(g * GQ, GQ)], start=(part == 0),
                                   stop=(part == 1))
                mm.then_inc(q_full, 1)

            def ring_free(base, p):
                if p >= 2:
                    pe.wait_ge(a_used, base + p - 1)

            def a_product(base, p, par, a):
                ring_free(base, p)
                qt, kc = a % QT, a // QT
                pe.matmul(ps_a[:, p % 2, :], q1[:, par, qt * P:(qt + 1) * P], kh[:, kc * 512:(kc + 1) * 512],
                          start=True, stop=True).then_inc(a_full, 1)

            def tap_product(base, p, par, k):
                ring_free(base, p)
                for part in range(2):
                    mm = pe.matmul(ps_a[:, p % 2, :], tapw[:, part, CENTER_FIRST[k], :, :], y[:, par, :],
                                   start=(part == 0), stop=(part == 1))
                mm.then_inc(a_full, 1)

            def k_product(base, p, im, c):
                ring_free(base, p)
                pe.wait_ge(xt_ready, KC * im + c + 1)
                for part in range(2):
                    mm = pe.matmul(ps_a[:, p % 2, :], wk_p[:, part, :], xT[:, c * 512:(c + 1) * 512],
                                   start=(part == 0), stop=(part == 1))
                mm.then_inc(a_full, 1)

            def logits_product(base, p, im, c):
                ring_free(base, p)
                pe.wait_ge(x2_ready, KC * im + c + 1)
                for n in range(4):
                    mm = pe.matmul(ps_a[:, p % 2, n * 2 * E:(n + 1) * 2 * E], y[:, c % 2, n * P:(n + 1) * P], gw_p[:],
                                   start=True, stop=True)
                mm.then_inc(a_full, 1)

            def count_product(base, p, im):
                ring_free(base, p)
                pe.wait_ge(cp_ready, im + 1)
                pe.matmul(ps_a[:, p % 2, 0:E], before[:], cum[:, 1, N - 1, :], start=True, stop=False)
                pe.matmul(ps_a[:, p % 2, 0:E], ones[:], carry[:], start=False, stop=True).then_inc(a_full, 1)

            def conv_product(im, i):
                pe.wait_ge(x_in, 64 * (im + 1))
                pe.matmul(ps_m[:], w1bd[:], xc[:, bass.ds(i * 512, 512)], start=True, stop=True).then_inc(conv1, 1)

            def transposed(c, full):
                for n in range(4):
                    mm = pe.transpose(ps_m[:, n * P:(n + 1) * P],
                                      xhl[:, 4 * c + n, :, :].rearrange("p t d -> p (t d)"), ident[:])
                mm.then_inc(full, 1)

            def max_rows(t):
                pe.wait_ge(max_ready, t + 1)
                pe.matmul(ps_m[D:D + QT, 0:P], rowmax[:], ident[:], start=True, stop=True).then_inc(mrow_full, 1)

            def start():
                pe.wait_ge(s_dset, 10)
                conv_product(0, 0)
                for i in range(PCH):
                    pe.wait_ge(y_ready, i + 1)
                    if i + 1 < PCH:
                        conv_product(0, i + 1)
                    for k in range(TAPS):
                        tap_product(0, i * TAPS + k, i % 2, k)
                pe.wait_ge(xn_ready, 1)
                transposed(0, xt_full)
                pe.wait_ge(xt_ready, 1)
                q_product(0, 0)
                pe.wait_ge(q_ready, 1)
                for c in range(KC + 1):
                    if c < KC:
                        if c >= 1:
                            pe.wait_ge(xt_ready, c + 1)
                        if c + 1 < KC:
                            transposed(c + 1, xt_full)
                        k_product(0, START_K[c], 0, c)
                    if c >= 1:
                        pe.wait_ge(kh_ready, c)
                        for i in range(QT):
                            a_product(0, START_A[c - 1] + i, 0, (c - 1) * QT + i)
                max_rows(0)

            def weigh(t0, j, part, im=None):
                src, ready = ((ph, ph_ready), (pl, pl_ready))[part]
                if im is not None and j % 4 == 0 and part == 0:
                    pe.wait_ge(xs_ready, 4 * im + j // 4 + 1)
                pe.wait_ge(ready, t0 + j + 1)
                for i in range(2):
                    mm = pe.matmul(ps_o[:], xs[:, 2 * j + i, :], src[:, j % RP, i * 512:(i + 1) * 512],
                                   start=(j == 0 and i == 0 and part == 0), stop=(j == STEPS - 1 and i == 1 and part == 1))
                if part:
                    mm.then_inc(av_done, 1)

            def project(t):
                pe.wait_ge(live_in, t + 1)
                for qt in range(QT):
                    mm = pe.matmul(ps_m[:, qt * (D + 2):(qt + 1) * (D + 2)], oT[:, qt * P:(qt + 1) * P], wg[:],
                                   start=True, stop=True)
                mm.then_inc(post_full, 1)

            def bank(im, g, par, kind, j, before_it):
                what = BANK[kind][j]
                t = im * G + g
                if what == "conv":
                    pe.wait_ge(mrow_ready, t + 1)
                    conv_product(im + 1, g - 1)
                    return
                if before_it is None:
                    wait_apart(pe, mrow_ready, t + 1)
                elif before_it == "conv":
                    pe.wait_ge(y_ready, PCH * (im + 1) + g)
                elif before_it == "q":
                    wait_apart(pe, q_ready, t + 2)
                elif before_it == "post":
                    wait_apart(pe, h_ready, t)
                elif kind == "keys":
                    wait_apart(pe, xt_ready, KC * (im + 1) + int(before_it[1]) + 1)
                else:
                    wait_apart(pe, x2_ready, KC * (im - 1) + int(before_it[1]) + 1)
                if what == "q":
                    if kind == "keys":
                        pe.wait_ge(xt_ready, KC * (im + 1) + 1)
                    q_product(t + 1, 0 if kind == "keys" else g + 1)
                elif what == "post":
                    project(t - 1)
                elif kind == "keys":
                    if what == "T0":
                        wait_apart(pe, xn_ready, im + 2)
                    transposed(int(what[1]), xt_full)
                else:
                    if what in ("T0", "T6"):
                        wait_apart(pe, x2_split, 2 * (im - 1) + 1 + (what == "T6"))
                    transposed(int(what[1]), x2_full)

            def ring(im, g, par, kind, base, p, what, n):
                nxt = im + 1 if kind == "keys" else im
                if what == "a":
                    if n == 0:
                        pe.wait_ge(q_ready, im * G + g + 2)
                    if kind == "keys" and n % QT == 0:
                        pe.wait_ge(kh_ready, KC * nxt + n // QT + 1)
                    a_product(base, p, 1 - par, n)
                elif what == "t":
                    if n == 0:
                        pe.wait_ge(y_ready, PCH * (im + 1) + g)
                    tap_product(base, p, 1 - par, n)
                elif what == "k":
                    k_product(base, p, nxt, n)
                elif what == "l":
                    logits_product(base, p, im - 1, n)
                else:
                    count_product(base, p, im - 1)

            def group(im, g, par, kind, base, more):
                t0 = (im * G + g) * STEPS
                first = isinstance(g, int) and g == 0
                last_bank = None
                for j in range(STEPS):
                    if j >= LAG:
                        lagged = (t0, j - LAG)
                    else:
                        lagged = None if first else (t0 - STEPS, STEPS - LAG + j)
                    pe.wait_ge(ph_ready, t0 + j - 1) if j >= 2 or not (first and kind == "plain") else None
                    here = list(entries(kind, j))
                    if j == 0:
                        for n in range(2):
                            pe.matmul(ps_s[:, n, :], kh[:, n * P:(n + 1) * P], q1[:, par, :], start=True, stop=False)
                        pe.wait_ge(mrow_ready, im * G + g + 1)
                    for i in range(4):
                        if i < 2:
                            n = 2 * j + i
                            dst = ps_s[:, 2 * (j % 2) + i, :]
                            if j > 0:
                                pe.matmul(dst, kh[:, n * P:(n + 1) * P], q1[:, par, :], start=True, stop=False)
                            mm = pe.matmul(dst, kl[:, n * P:(n + 1) * P], q2[:, par, :], start=False, stop=True)
                            if i == 1:
                                mm.then_inc(s_full, 1)
                            if i == 1 and j == 0 and -1 in BANK[kind]:
                                bank(im, g, par, kind, -1, None)
                                last_bank = BANK[kind][-1]
                        elif lagged is not None:
                            if j == LAG and i == 2 and not first:
                                pe.wait_ge(oT_ready, im * G + g)
                            weigh(*lagged, i - 2, im if first else None)
                        if i == 1 and j in BANK[kind] and not (BANK[kind][j] == "post" and kind == "plain" and first):
                            bank(im, g, par, kind, j, last_bank)
                            last_bank = BANK[kind][j]
                        if i < len(here):
                            p, what, n = here[i]
                            ring(im, g, par, kind, base, p, what, n)
                    for p, what, n in here[4:]:
                        ring(im, g, par, kind, base, p, what, n)
                    if kind == "logits" and j == CHOOSE:
                        max_rows(im * G + g + 1)
                if kind == "keys":
                    here = list(entries(kind, STEPS))
                    for i in range(2 * LAG):
                        weigh(t0, STEPS - LAG + i // 2, i % 2)
                        if i < len(here):
                            p, what, n = here[i]
                            ring(im, g, par, kind, base, p, what, n)
                if kind not in ("last", "logits"):
                    max_rows(im * G + g + 1)
                if kind == "logits":
                    for p, what, n in entries(kind, STEPS):
                        ring(im, g, par, kind, base, p, what, n)

            def finish(base):
                t0 = (B * G - 1) * STEPS
                for i in range(2 * LAG):
                    weigh(t0, STEPS - LAG + i // 2, i % 2)
                pe.wait_ge(h_ready, B * G - 1)
                project(B * G - 1)
                for c in range(KC):
                    if c == 0:
                        pe.wait_ge(h_ready, B * G)
                        pe.wait_ge(x2_split, 2 * B - 1)
                    else:
                        pe.wait_ge(x2_ready, KC * (B - 1) + c)
                    if c == 6:
                        pe.wait_ge(x2_split, 2 * B)
                    transposed(c, x2_full)
                    if c >= 1:
                        logits_product(base, c - 1, B - 1, c - 1)
                logits_product(base, KC - 1, B - 1, KC - 1)
                count_product(base, KC, B - 1)

            stream(pe, start, group, finish)

            with pe.Fori(0, E // 2) as pair:
                def turn_in(c):
                    k = pair * (2 * CH) + c
                    wait_apart(pe, xmhl_ready, k + 1)
                    for i in range(4):
                        mm = pe.transpose(ps_a[:, c % 2, i * P:(i + 1) * P],
                                          xmhl[:, i, :, :].rearrange("p t d -> p (t d)"), ident[:])
                    mm.then_inc(xmT_full, 1)

                def hidden(c):
                    k = pair * (2 * CH) + c
                    if c % CH == 0:
                        pe.wait_ge(w_ready, pair * 2 + c // CH + 1)
                    pe.wait_ge(xmT_ready, k + 1)
                    for f in range(FC):
                        for part in range(2):
                            mm = pe.matmul(ps_s[:, 2 * (c % 2) + f, :], w1p[:, c // CH, part, f * P:(f + 1) * P],
                                           xmT[:, c % 2, :], start=(part == 0), stop=(part == 1))
                        mm.then_inc(hid_full, 1)

                def result(c):
                    k = pair * (2 * CH) + c
                    pe.wait_ge(hid_a, k + 1)
                    pe.wait_ge(hid_b, k + 1)
                    for f in range(FC):
                        mm = pe.matmul(ps_o[0:D, :], w2s[:, c // CH, f, :], hid[:, c % 2, f, :],
                                       start=(f == 0), stop=(f == 1))
                    mm.then_inc(yT_full, 1)

                def turn_out(c):
                    k = pair * (2 * CH) + c
                    wait_apart(pe, yT_ready, k + 1)
                    wait_apart(pe, ym_read, k + XR)
                    for i in range(4):
                        mm = pe.transpose(ps_m[:, i * D:(i + 1) * D], yT[c % 2][:, i * P:(i + 1) * P], ident[0:D, 0:D])
                    mm.then_inc(ym_full, 1)

                turn_in(0)
                for c in range(2 * CH):
                    if c + 1 < 2 * CH:
                        turn_in(c + 1)
                    hidden(c)
                    if c >= 1:
                        turn_out(c - 1)
                    result(c)
                turn_out(2 * CH - 1)

        @block.scalar
        def _(act):
            act.wait_ge(made, 6)
            for q in range(FILLS):
                act.dma_start(slots_x[q * FR * P:(q + 1) * FR * P, :].rearrange("(p a) d -> p a d", p=P),
                              fill).then_inc(zero_out, 16)
            act.wait_ge(s_dset, 2)
            act.activation(bn_t[:, 1:2], bn_t[:, 0:1], ACT.Sqrt).then_inc(s_aset, 1)

            def relu(im, i, par):
                act.wait_ge(conv1, PCH * im + i + 1)
                act.activation(y[:, par, :], ps_m[:], ACT.Relu,
                               bias=bn_bias[:], scale=bn_scale[:]).then_inc(y_high, 1)

            def root(nth, a, b):
                act.wait_ge(var_ready, nth + 1)
                act.activation(sd[:, a:b], var[:, a:b], ACT.Sqrt).then_inc(sd_ready, 1)

            def take_xT(im, c):
                act.wait_ge(xt_full, im * KC + c + 1)
                act.activation(xT[:, c * 512:(c + 1) * 512], ps_m[:], ACT.Copy).then_inc(xt_ready, 1)

            def take_x2(im, c, base, places):
                if c >= 2:
                    wait_apart(act, a_full, base + places[c - 2] + 1)
                act.wait_ge(x2_full, im * KC + c + 1)
                act.activation(y[:, c % 2, :], ps_m[:], ACT.Copy).then_inc(x2_ready, 1)

            def take_k(im, base, p, c):
                act.wait_ge(a_full, base + p + 1)
                act.activation(kh[:, c * 512:(c + 1) * 512], ps_a[:, p % 2, :], ACT.Identity,
                               bias=bk2[:]).then_inc(kh_ready, 1)

            def take_q(t, par):
                act.wait_ge(q_full, t + 1)
                act.activation(q2[0:D, par, :], ps_m[0:D, :], ACT.Identity, bias=bq2[0:D, :])
                act.activation(q1[:, par, :], ps_m[:], ACT.Identity, bias=bq2[:]).then_inc(qh_ready, 1)

            def take_o(t):
                act.wait_ge(av_done, (t + 1) * STEPS)
                act.activation(oT[:], ps_o[:], ACT.Copy).then_inc(oT_ready, 1)

            def exp_logits(im):
                act.wait_ge(lg_centred, im + 1)
                act.activation(lg_e, lg[:], ACT.Exp).then_inc(lg_exp, 1)

            def start():
                act.wait_ge(s_dset, 9)
                for i in range(PCH):
                    relu(0, i, i % 2)
                root(0, 0, N)
                take_xT(0, 0)
                take_q(0, 0)
                for c in range(KC):
                    if c + 1 < KC:
                        take_xT(0, c + 1)
                    take_k(0, 0, START_K[c], c)

            def bank(im, g, par, kind, j, base):
                what = BANK[kind][j]
                if what == "conv":
                    relu(im + 1, g - 1, 1 - par)
                elif what == "q":
                    take_q(im * G + g + 1, 1 - par)
                elif what != "post" and kind == "keys":
                    take_xT(im + 1, int(what[1]))
                elif what != "post":
                    take_x2(im - 1, int(what[1]), base,
                            [p for jj in range(STEPS) for p, w, _ in entries(kind, jj) if w == "l"])

            def group(im, g, par, kind, base, more):
                t0 = (im * G + g) * STEPS
                first = isinstance(g, int) and g == 0
                for j in range(STEPS):
                    act.wait_ge(s_full, t0 + j + 1)
                    if j >= R32 or not (first and kind == "plain"):
                        act.wait_ge(pl_ready, t0 + j - R32 + 1)
                    act.activation(p32[:, j % R32, :], ps_s[:, 2 * (j % 2):2 * (j % 2) + 2, :], ACT.Exp, scale=SCALE)
                    if j == 0 and -1 in BANK[kind]:
                        bank(im, g, par, kind, -1, base)
                    if j >= RP or not (first and kind == "plain"):
                        act.wait_ge(av_done, t0 + j - RP + 1)
                    act.activation(ph[:, j % RP, :], ps_s[:, 2 * (j % 2):2 * (j % 2) + 2, :], ACT.Exp,
                                   scale=SCALE).then_inc(ph_ready, 1)
                    if j in BANK[kind]:
                        bank(im, g, par, kind, j, base)
                    for p, what, n in entries(kind, j):
                        if what == "k":
                            take_k(im + 1, base, p, n)
                    if j == LAG - 1 and not first:
                        take_o(im * G + g - 1)
                    if kind == "root" and j == 8:
                        root(2 * im + 1, 0 if more else N, N + 24)
                    if kind == "logits" and j == 4:
                        root(2 * im, N + 24, 2 * N)
                if kind == "keys":
                    for p, what, n in entries(kind, STEPS):
                        if what == "k":
                            take_k(im + 1, base, p, n)
                    take_o(im * G + g)
                if kind == "logits":
                    exp_logits(im - 1)

            def finish(base):
                take_o(B * G - 1)
                root(2 * B, N + 24, 2 * N)
                for c in range(KC):
                    take_x2(B - 1, c, base, list(range(KC)))
                exp_logits(B - 1)

            stream(act, start, group, finish)

            with act.Fori(0, E // 2) as pair:
                def take_xm(c):
                    act.wait_ge(xmT_full, pair * (2 * CH) + c + 1)
                    act.activation(xmT[:, c % 2, :], ps_a[:, c % 2, :], ACT.Copy).then_inc(xmT_ready, 1)

                take_xm(0)
                for c in range(2 * CH):
                    k = pair * (2 * CH) + c
                    e = pair * 2 + c // CH
                    if c + 1 < 2 * CH:
                        take_xm(c + 1)
                    wait_apart(act, hid_full, (k + 1) * 2 - 1)
                    if c >= 2:
                        wait_apart(act, yT_full, k - 1)
                    act.activation(hid[:, c % 2, 0, :], ps_s[:, 2 * (c % 2), :], ACT.Relu,
                                   bias=b1c[:, bass.ds(e, 1), 0:1].rearrange("p a b -> p (a b)")).then_inc(hid_a, 1)
                    wait_apart(act, yT_full, k + 1)
                    act.activation(yT[c % 2], ps_o[0:D, :], ACT.Identity, bias=b2c[:, bass.ds(e, 1)]).then_inc(yT_ready, 1)

        @block.vector
        def _(dve):
            dve.memset(carry[:], 0.0)
            dve.memset(xh[:, 0:1, :], 0.0)
            dve.memset(xh[:, RH + 1:RH + 2, :], 0.0)
            dve.memset(kl[D:P, :].bitcast(F32), 0.0)
            dve.memset(q2[D:P, :, :].bitcast(F32), 0.0)
            tap32 = p32[:].rearrange("p a b -> p (a b)")[:, 0:TAPS * P].rearrange("p (k c h) -> p k c h", k=TAPS, h=2)
            dve.memset(xs[:], 0.0)
            dve.memset(tap32, 0.0).then_inc(cleared, 1)
            dve.wait_ge(cleared, 1)
            dve.memset(kl[D:D + QT, :].bitcast(F32), 1.0)
            dve.sem_inc(ym_read, XR)
            dve.sem_inc(w_free, 1)
            dve.sem_inc(ym_free, XR)

            setup = Order(dve, s_dset, 0)
            dve.wait_ge(consts_in, 16 * N_CONST)
            dve.wait_ge(made, 11)
            dve.wait_ge(s_pset, 1)
            dve.tensor_copy(wq_t[:], ps_m[:, 0:D].unsqueeze(1).to_broadcast([P, 2, D]))
            dve.tensor_copy(wk_t[:], ps_m[:, D:2 * D].unsqueeze(1).to_broadcast([P, 2, D]))
            dve.tensor_copy(wg[:, D:D + 2], ident[:, 63:65])
            dve.tensor_scalar(own[D:D + QT, :, :], ident[D:D + QT, D:D + QT].unsqueeze(2).to_broadcast([QT, QT, P]),
                              -1.0, None, ALU.mult)
            dve.tensor_copy(woT[:], ps_m[0:D, 2 * D:3 * D])
            dve.tensor_scalar(wvx[:, 0:63], w_nat[:, 2, 0, 0:63], w_nat[:, 2, 0, 63:64], None, ALU.subtract)
            setup.did(dve.tensor_scalar(wvx[:, 65:128], w_nat[:, 2, 0, 0:63], w_nat[:, 2, 0, 63:64], None, ALU.subtract))
            dve.memset(xs[:, :, 63:64], 1.0)
            setup.did(dve.tensor_scalar(bn_t[:, 0:1], bn_raw[:, 4:5], BN_EPS, None, ALU.add))
            dve.tensor_tensor(bn_t[:, 3:4], bn_raw[:, 0:1], bn_raw[:, 3:4], ALU.subtract)
            setup.then(dve.tensor_tensor(bn_raw[:, 2:3], bn_raw[:, 2:3], ident[:, CR:CR + 1], ALU.add))
            setup.then(dve.tensor_tensor(bn_raw[:, 2:3], bn_raw[:, 2:3], ident[:, 32 + CR:33 + CR], ALU.add))
            dve.wait_ge(s_aset, 1)
            setup.then(dve.reciprocal(bn_t[:, 2:3], bn_t[:, 1:2]))
            setup.then(dve.tensor_tensor(bn_scale[:], bn_raw[:, 1:2], bn_t[:, 2:3], ALU.mult))
            for low in range(2):
                for half in range(2):
                    rows = slice(64 * low + 32 * half, 64 * low + 32 * half + CR + 1)
                    ins = dve.tensor_copy(tap32[rows, :, :, half],
                                          cw2[rows, :].unsqueeze(2).to_broadcast([CR + 1, TAPS, C]))
            setup.then(ins)
            dve.tensor_copy(tapw[:, 0], tap32)
            dve.tensor_copy(wq_p[:, 0, :], wq_t[:].rearrange("p a b -> p (a b)"))
            dve.tensor_copy(wk_p[:, 0, :], wk_t[:].rearrange("p a b -> p (a b)"))
            setup.then(dve.tensor_copy(gw_p[:, 0, :], gw[:]))
            dve.tensor_tensor(tapw[:, 1], tap32, tapw[:, 0].bitcast(F32), ALU.subtract)
            dve.tensor_tensor(wq_p[:, 1, :], wq_t[:].rearrange("p a b -> p (a b)"), wq_p[:, 0, :].bitcast(F32), ALU.subtract)
            dve.tensor_tensor(wk_p[:, 1, :], wk_t[:].rearrange("p a b -> p (a b)"), wk_p[:, 0, :].bitcast(F32), ALU.subtract)
            dve.tensor_tensor(gw_p[:, 1, :], gw[:], gw_p[:, 0, :].bitcast(F32), ALU.subtract)
            dve.scalar_tensor_tensor(out=bn_bias[:], in0=bn_t[:, 3:4], scalar=bn_scale[:], in1=bn_raw[:, 2:3],
                                     op0=ALU.mult, op1=ALU.add).then_inc(s_dset, 1)
            dve.wait_ge(s_pset, 2)
            dve.tensor_copy(wg[:, 0:D], ps_m[:, 256:256 + D]).then_inc(s_dset, 1)

            dve.sem_inc(h_free, 1)

            def spread(v, n0, n1):
                return v.unsqueeze(2).to_broadcast([P, n1 - n0, D])

            def ln_place(which, n0, n1):
                return (xcen[:, n0:n1, :], xw[:, n0:n1, 0:D])[which]

            def ln_mean(order, im, which, n0, n1):
                src = h[:, bass.ds(im % 2 * N + n0, n1 - n0), :]
                order.then(dve.tensor_reduce(ln_s[:, which, 0, n0:n1], src, AX.X, ALU.add))
                order.then(dve.tensor_scalar(ln_s[:, which, 1, n0:n1], ln_s[:, which, 0, n0:n1], 1.0 / D, None, ALU.mult))

            def ln_centre(order, im, which, n0, n1):
                src = h[:, bass.ds(im % 2 * N + n0, n1 - n0), :]
                order.then(dve.tensor_tensor(ln_place(which, n0, n1), src, spread(ln_s[:, which, 1, n0:n1], n0, n1), ALU.subtract))

            def ln_squares(order, which, n0, n1):
                v = ln_place(which, n0, n1)
                if which == 0:
                    scratch = xhl[:, n0:n1, 0, :]
                else:
                    scratch = tmp[:].rearrange("p a r w -> p (a r) w")[:, 0:n1 - n0, :]
                order.then(dve.tensor_tensor(scratch, v, v, ALU.mult))
                order.then(dve.tensor_reduce(ln_q[:, which, n0:n1], scratch, AX.X, ALU.add))
                order.then(dve.tensor_scalar(var[:, which * N + n0:which * N + n1], ln_q[:, which, n0:n1], 1.0 / D, LN_EPS,
                                             ALU.mult, ALU.add))

            def ln_scale(order, which, n0, n1):
                v = ln_place(which, n0, n1)
                order.then(dve.reciprocal(ln_s[:, which, 2, n0:n1], sd[:, which * N + n0:which * N + n1]))
                order.then(dve.tensor_tensor(v, v, spread(ln_s[:, which, 2, n0:n1], n0, n1), ALU.mult))

            def ln_high(order, which, n0, n1):
                order.then(dve.tensor_copy(xhl[:, n0:n1, 0, :].bitcast(F32R), ln_place(which, n0, n1)))

            def ln_low(which, n0, n1, ready):
                dve.tensor_tensor(xhl[:, n0:n1, 1, :].bitcast(F32R), ln_place(which, n0, n1), xhl[:, n0:n1, 0, :],
                                  ALU.subtract).then_inc(ready, 1)

            ND_LN1, ND_LN2 = 9, 24

            def ln1(im, at):
                return Order(dve, s_ln1, im * ND_LN1 + at)

            def ln2(im, at):
                return Order(dve, s_ln2, im * ND_LN2 + at)

            def cast_xs(im, i):
                quarter = slice(8 * i, 8 * i + 8)
                order = Order(dve, s_cast, im * 4 + i)
                order.then(dve.tensor_copy(xs[:, quarter, 0:63], xcen[:, quarter, 0:63]))
                dve.tensor_tensor(xs[:, quarter, 65:128], xcen[:, quarter, 0:63], xs[:, quarter, 0:63],
                                  ALU.subtract).then_inc(xs_ready, 1)

            def low_y(im, i, par):
                dve.wait_ge(y_high, PCH * im + i + 1)
                order = Order(dve, s_tap, (im * PCH + i) * ND1)
                order.then(dve.tensor_scalar(y32[D:P, :], ps_m[D:P, :], bn_scale[D:P, :], bn_bias[D:P, :],
                                             ALU.mult, ALU.add))
                dve.scalar_tensor_tensor(out=y[D:P, par, :], in0=y32[D:P, :], scalar=0.0,
                                         in1=y[D:P, par, :].bitcast(F32),
                                         op0=ALU.max, op1=ALU.subtract).then_inc(y_ready, 1)

            products = (tmp[:, 0, :, :], tmp[:, 1, :, :], y32[:].rearrange("p (r w) -> p r w", w=WW))

            def tap_columns(kk):
                dc = CENTER_FIRST[kk] % 3 - 1
                return max(0, -dc), min(WW, WW - dc)

            def tap(im, i, base, p, kk, entry_before=None):
                mine = h[:, bass.ds(im % 2 * N + i * 8, 8), :]
                k = CENTER_FIRST[kk]
                dr, dc = k // 3, k % 3 - 1
                w0, w1_ = tap_columns(kk)
                wd = ps_a[:, p % 2, :].rearrange("p (r w) -> p r w", w=WW)[:, :, w0:w1_]
                src = xh[:, bass.ds(i * 8 + dr, 8), w0 + dc:w1_ + dc]
                if kk == 0:
                    dve.wait_ge(x_in, 64 * (im + 1))
                dve.wait_ge(a_full, base + p + 1)
                if kk == 0:
                    dve.tensor_tensor(mine, wd, src, ALU.mult).then_inc(a_used, 1)
                else:
                    if kk == 2:
                        dve.wait_ge(y_ready, PCH * im + i + 1)
                    if kk >= 4:
                        Order(dve, s_tap, (im * PCH + i) * ND1 + 1).need(kk - 3)
                    dve.tensor_tensor(products[kk % 3][:, :, w0:w1_], wd, src, ALU.mult).then_inc(a_used, 1)
                if kk >= 2:
                    add_tap(im, i, kk - 1, entry_before)
                if kk == TAPS - 1:
                    add_tap(im, i, kk, base + p + 1)
                    order = Order(dve, s_tap, (im * PCH + i) * ND1)
                    order.need(ND1)
                    dve.sem_inc(x_free, 1)
                return base + p + 1

            def add_tap(im, i, kk, used):
                w0, w1_ = tap_columns(kk)
                mine = h[:, bass.ds(im % 2 * N + i * 8, 8), w0:w1_]
                order = Order(dve, s_tap, (im * PCH + i) * ND1 + 1 + kk - 1)
                dve.wait_ge(a_used, used)
                if kk >= 2:
                    order.need(0)
                order.did(dve.tensor_tensor(mine, mine, products[kk % 3][:, :, w0:w1_], ALU.add))

            def low_k(im, base, p, c):
                dve.wait_ge(kh_ready, KC * im + c + 1)
                dve.scalar_tensor_tensor(out=kl[0:D, c * 512:(c + 1) * 512], in0=ps_a[0:D, p % 2, :],
                                         scalar=bk2[0:D, :], in1=kh[0:D, c * 512:(c + 1) * 512].bitcast(F32),
                                         op0=ALU.add, op1=ALU.subtract).then_inc(a_used, 1)

            def reduce_a(base, p, a):
                dve.wait_ge(a_full, base + p + 1)
                dve.tensor_reduce(mx[:, a % QT, a // QT:a // QT + 1], ps_a[:, p % 2, :], AX.X, ALU.max).then_inc(a_used, 1)

            def whole_max(t, used):
                dve.wait_ge(a_used, used)
                dve.tensor_reduce(rowmax[:], mx[:], AX.X, ALU.max).then_inc(max_ready, 1)

            def take_max(t, par):
                dve.wait_ge(mrow_full, t + 1)
                dve.scalar_tensor_tensor(
                    out=q2[D:D + QT, par, :].rearrange("p (q c) -> p q c", q=QT),
                    in0=ps_m[D:D + QT, 0:P].unsqueeze(1).to_broadcast([QT, QT, P]), scalar=LIFT,
                    in1=own[D:D + QT, :, :], op0=ALU.subtract, op1=ALU.mult).then_inc(mrow_ready, 1)

            def low_q(t, par):
                dve.wait_ge(qh_ready, t + 1)
                dve.scalar_tensor_tensor(out=q1[D:P, par, :], in0=ps_m[D:P, :], scalar=bq2[D:P, :],
                                         in1=q1[D:P, par, :].bitcast(F32), op0=ALU.add, op1=ALU.subtract)
                dve.tensor_scalar(live_q[D:D + 1, :], ps_m[D:D + 1, :], bq2[D:D + 1, :], 0.0,
                                  ALU.add, ALU.not_equal).then_inc(q_ready, 1)

            def new_live(t, g, par):
                dve.wait_ge(q_ready, t + 1)
                dve.scalar_tensor_tensor(out=live[D:D + 1, par, :], in0=kh[D:D + 1, bass.ds(g * GQ, GQ)].bitcast(F32), scalar=0.0,
                                         in1=live_q[D:D + 1, :], op0=ALU.not_equal, op1=ALU.mult).then_inc(live_ready, 1)

            def mask_row(t, par):
                dve.wait_ge(live_ready, t + 1)
                dve.wait_ge(oT_ready, t + 1)
                dve.tensor_copy(oT[D:D + 1, :], live[D:D + 1, par, :]).then_inc(live_in, 1)

            def residual(im, g):
                order = Order(dve, s_dve2, (im * G + g) * ND2)
                mine = h[:, bass.ds(im % 2 * N + g * QT, QT), :]
                dve.wait_ge(post_full, im * G + g + 1)
                got_o = ps_m[:, 0:QT * (D + 2)].rearrange("p (q d) -> p q d", d=D + 2)
                order.then(dve.reciprocal(post[:, 0, :], got_o[:, :, D:D + 1].rearrange("p q a -> p (q a)")))
                order.then(dve.tensor_tensor(post[:, 1, :], post[:, 0, :],
                                             got_o[:, :, D + 1:D + 2].rearrange("p q a -> p (q a)"), ALU.mult))
                order.then(dve.tensor_tensor(att[:], got_o[:, :, 0:D],
                                             post[:, 1, :].unsqueeze(2).to_broadcast([P, QT, D]), ALU.mult))
                order.then(dve.tensor_tensor(att[:], att[:], bo_all[:].unsqueeze(1).to_broadcast([P, QT, D]), ALU.add))
                dve.tensor_tensor(mine, mine, att[:], ALU.add).then_inc(h_ready, 1)
                assert order.n == ND2
                wait_apart(dve, h_ready, im * G + g + 1)

            def over_e(v):
                return v.unsqueeze(2).to_broadcast([P, N, E])

            def over_n(v):
                return v.unsqueeze(1).to_broadcast([P, N, E])

            def take_logits(base, p, c):
                wait_apart(dve, a_full, base + p + 1)
                dve.tensor_reduce(lg[:, 4 * c:4 * c + 4, :], ps_a[:, p % 2, 0:8 * E].rearrange("p (n t e) -> p n e t", e=E, t=2),
                                  AX.X, ALU.add).then_inc(a_used, 1)

            def choose(im):
                order = Order(dve, s_dve3, im * ND3)
                order.then(dve.tensor_tensor(lg[:], lg[:], over_n(gb_all[:]), ALU.add))
                order.then(dve.tensor_reduce(rt[:, 0, :], lg[:], AX.X, ALU.max))
                order.then(dve.tensor_tensor(oneh[:], lg[:], over_e(rt[:, 0, :]), ALU.is_equal))
                order.then(dve.tensor_tensor(oneh[:], oneh[:], over_n(e_down[:]), ALU.mult))
                order.then(dve.tensor_reduce(rt[:, 1, :], oneh[:], AX.X, ALU.max))
                dve.tensor_tensor(lg[:], lg[:], over_e(rt[:, 0, :]), ALU.subtract).then_inc(lg_centred, 1)
                order.then(dve.tensor_tensor(oneh[:], oneh[:], over_e(rt[:, 1, :]), ALU.is_equal))
                order.then(dve.tensor_copy(cum[:, 0, :, :], oneh[:]))
                src = 0
                for s in (1, 2, 4, 8, 16):
                    order.did(dve.tensor_copy(cum[:, 1 - src, 0:s, :], cum[:, src, 0:s, :]))
                    ins = dve.tensor_tensor(cum[:, 1 - src, s:N, :], cum[:, src, s:N, :], cum[:, src, 0:N - s, :], ALU.add)
                    src = 1 - src
                    if s < 16:
                        order.then(ins)
                    else:
                        ins.then_inc(cp_ready, 1)
                assert order.n == 16, order.n

            def places(im, base, p):
                order = Order(dve, s_dve3, im * ND3 + 16)
                wts = xw[:, :, D:D + 1].rearrange("p n a -> p (n a)")
                numbers = xw[:, :, D + 1:D + 2].rearrange("p n a -> p (n a)")
                wait_apart(dve, lg_exp, im + 1)
                order.then(dve.tensor_reduce(rt[:, 2, :], lg_e, AX.X, ALU.add))
                order.did(dve.reciprocal(rt[:, 3, :], rt[:, 2, :]))
                dve.wait_ge(a_full, base + p + 1)
                order.did(dve.tensor_tensor(carry[:], carry[:], cum[:, 1, N - 1, :], ALU.add))
                dve.tensor_copy(cbase[:], ps_a[:, p % 2, 0:E]).then_inc(a_used, 1)
                dve.wait_ge(a_used, base + p + 1)
                order.then(dve.tensor_tensor(cum[:, 0, :, :], cum[:, 1, :, :], over_n(cbase[:]), ALU.add))
                order.then(dve.tensor_tensor(cum[:, 0, :, :], cum[:, 0, :, :], oneh[:], ALU.mult))
                order.did(dve.tensor_reduce(rt[:, 4, :], cum[:, 0, :, :], AX.X, ALU.add))
                order.then(dve.tensor_tensor(oneh[:], oneh[:], over_n(e_base[:]), ALU.mult))
                order.then(dve.tensor_reduce(rt[:, 5, :], oneh[:], AX.X, ALU.add))
                order.then(dve.tensor_scalar(rt[:, 0, :], rt[:, 4, :], float(CAP), None, ALU.is_le))
                order.did(dve.tensor_tensor(wts, rt[:, 3, :], rt[:, 0, :], ALU.mult))
                order.did(dve.tensor_scalar(rt[:, 1, :], rt[:, 0, :], -4.0 * E * CAP, 4.0 * E * CAP, ALU.mult, ALU.add))
                order.did(dve.tensor_copy(numbers, token[:]))
                order.then(dve.tensor_scalar(rt[:, 2, :], rt[:, 4, :], -1.0, None, ALU.add))
                order.then(dve.tensor_tensor(rt[:, 2, :], rt[:, 2, :], rt[:, 5, :], ALU.add))
                order.did(dve.tensor_scalar(token[:], token[:], float(S), None, ALU.add))
                dve.tensor_tensor(put_at[:], rt[:, 2, :], rt[:, 1, :], ALU.add).then_inc(put_ready, 1)
                assert order.n == ND3 - 16, order.n

            def start():
                for i in range(PCH):
                    low_y(0, i, i % 2)
                    entry = None
                    for kk in range(TAPS):
                        entry = tap(0, i, 0, i * TAPS + kk, kk, entry)
                dve.wait_ge(zero_out, 16 * FILLS)
                o = ln1(0, 0)
                ln_mean(o, 0, 0, 0, N)
                ln_centre(o, 0, 0, 0, N)
                ln_squares(o, 0, 0, N)
                dve.sem_inc(var_ready, 1)
                dve.wait_ge(sd_ready, 1)
                ln_scale(o, 0, 0, N)
                ln_high(o, 0, 0, N)
                ln_low(0, 0, N, xn_ready)
                assert o.n == ND_LN1, o.n
                low_q(0, 0)
                for c in range(KC + 1):
                    if c < KC:
                        low_k(0, 0, START_K[c], c)
                    if c == 0:
                        new_live(0, 0, 0)
                    else:
                        for i in range(QT):
                            reduce_a(0, START_A[c - 1] + i, (c - 1) * QT + i)
                whole_max(0, START)
                take_max(0, 0)
                for i in range(4):
                    cast_xs(0, i)

            def between(im, g, par, kind, more, j):
                t0 = (im * G + g) * STEPS
                if kind == "norm":
                    if more and j == 0:
                        ln_mean(ln1(im + 1, 0), im + 1, 0, 0, N)
                    if more and j == 1:
                        ln_centre(ln1(im + 1, 2), im + 1, 0, 0, N)
                    if more and j == 2:
                        ln_squares(ln1(im + 1, 3), 0, 0, N)
                    if j == 10:
                        wait_apart(dve, put_done, 16 * EARLY * (im + 1))
                        ln_mean(ln2(im, 0), im, 1, 0, 16)
                        ln_centre(ln2(im, 2), im, 1, 0, 16)
                    if j == 13:
                        ln_squares(ln2(im, 3), 1, 0, 16)
                elif kind == "root":
                    if j == 6:
                        ln_mean(ln2(im, 6), im, 1, 16, 24)
                        ln_centre(ln2(im, 8), im, 1, 16, 24)
                        ln_squares(ln2(im, 9), 1, 16, 24)
                        dve.sem_inc(var_ready, 1)
                    if j == 9:
                        dve.wait_ge(sd_ready, 2 * im + 2)
                        if more:
                            ln_scale(ln1(im + 1, 6), 0, 0, N)
                    if more and j == 10:
                        ln_high(ln1(im + 1, 8), 0, 0, N)
                    if more and j == 11:
                        ln_low(0, 0, N, xn_ready)
                    if not more and j == 12:
                        ln_scale(ln2(im, 12), 1, 0, 24)
                elif kind == "keys":
                    if j == 0:
                        ln_scale(ln2(im, 12), 1, 0, 24)
                    for i, at in enumerate((8, 12, 15)):
                        if j == at:
                            dve.wait_ge(av_done, t0 + 4 * (i + 1))
                            cast_xs(im + 1, i)
                    if j == 13:
                        dve.wait_ge(xt_full, KC * (im + 2))
                        ln_high(ln2(im, 14), 1, 0, 24)
                    if j == 14:
                        ln_low(1, 0, 24, x2_split)
                elif kind == "last":
                    if j == 8:
                        ln_high(ln2(im, 14), 1, 0, 24)
                        ln_low(1, 0, 24, x2_split)
                elif kind == "logits":
                    if j == 2:
                        rest_var(im - 1)
                    if j == 6:
                        rest_scale(im - 1)

            def rest_var(im):
                wait_apart(dve, put_late, 16 * (N - EARLY) * (im + 1))
                ln_mean(ln2(im, 15), im, 1, 24, N)
                ln_centre(ln2(im, 17), im, 1, 24, N)
                ln_squares(ln2(im, 18), 1, 24, N)
                dve.sem_inc(var_ready, 1)

            def rest_scale(im):
                dve.wait_ge(sd_ready, 2 * im + 3)
                o = ln2(im, 21)
                ln_scale(o, 1, 24, N)
                ln_high(o, 1, 24, N)
                ln_low(1, 24, N, x2_split)
                assert 21 + o.n == ND_LN2, o.n

            def group(im, g, par, kind, base, more):
                t = im * G + g
                first = isinstance(g, int) and g == 0
                after = im + 1 if kind == "keys" else im
                q_at = {"plain": 0, "norm": 0, "root": 0, "taps": 3, "keys": 2, "logits": 1, "last": None}[kind]
                post_at = [j for j in BANK[kind] if BANK[kind][j] == "post"][0]
                if kind == "logits":
                    residual(im - 1, G - 1)
                if kind == "taps":
                    dve.wait_ge(h_free, im + 1)
                    low_y(im + 1, g - 1, 1 - par)

                tap_entry = [None]

                def ring(p, what, n):
                    if what == "a":
                        reduce_a(base, p, n)
                    elif what == "t":
                        tap_entry[0] = tap(im + 1, g - 1, base, p, n, tap_entry[0])
                    elif what == "k":
                        low_k(im + 1, base, p, n)
                    elif what == "l":
                        take_logits(base, p, n)

                for j in range(STEPS):
                    between(im, g, par, kind, more, j)
                    if kind == "logits" and j == CHOOSE:
                        whole_max(t + 1, base + count[kind] - 1)
                        choose(im - 1)
                        take_max(t + 1, 1 - par)
                        places(im - 1, base, count[kind] - 1)
                        return
                    if j == q_at:
                        low_q(t + 1, 1 - par)
                        if first:
                            new_live(t + 1, g + 1, 1 - par)
                    if j == LAG + 1 and not first:
                        mask_row(t - 1, 1 - par)
                    if j == post_at and not first:
                        residual(im, g - 1)
                        if kind != "last":
                            new_live(t + 1, 0 if kind == "keys" else g + 1, 1 - par)
                    for p, what, n in entries(kind, j):
                        ring(p, what, n)
                if kind == "keys":
                    for p, what, n in entries(kind, STEPS):
                        ring(p, what, n)
                    mask_row(t, par)
                if kind == "last":
                    return
                whole_max(t + 1, base + count[kind])
                take_max(t + 1, 1 - par)
                if kind == "keys":
                    dve.wait_ge(av_done, (t + 1) * STEPS)
                    cast_xs(im + 1, 3)

            def finish(base):
                mask_row(B * G - 1, 1)
                residual(B - 1, G - 1)
                rest_var(B - 1)
                rest_scale(B - 1)
                for c in range(KC):
                    take_logits(base, c, c)
                wait_apart(dve, a_used, base + KC)
                choose(B - 1)
                places(B - 1, base, KC)

            stream(dve, start, group, finish)

            with dve.Fori(0, E // 2) as pair:
                order = Order(dve, s_dve4, pair * ND4)

                def parts(c):
                    k = pair * (2 * CH) + c
                    wait_apart(dve, xm_in[c % XR], (pair * 2 + c // XR + 1) * 16)
                    if c >= 1:
                        wait_apart(dve, xmT_full, k)
                    order.then(dve.tensor_copy(xmhl[:, :, 0, :].bitcast(F32R), xm[:, c % XR, :, 0:D]))
                    dve.tensor_tensor(xmhl[:, :, 1, :].bitcast(F32R), xm[:, c % XR, :, 0:D], xmhl[:, :, 0, :],
                                      ALU.subtract).then_inc(xmhl_ready, 1)

                def to_add(c):
                    k = pair * (2 * CH) + c
                    rows = ym[:, c % XR, :, :]
                    wait_apart(dve, ym_free, k + 1)
                    wait_apart(dve, ym_full, k + 1)
                    dve.tensor_copy(add_at[:, c % XR, :], xm[:, c % XR, :, D + 1:D + 2].rearrange("p a b -> p (a b)"))
                    dve.tensor_tensor(rows, ps_m[:, 0:4 * D].rearrange("p (a d) -> p a d", d=D),
                                      xm[:, c % XR, :, D:D + 1].to_broadcast([P, 4, D]), ALU.mult).then_inc(ym_read, 1)
                    dve.wait_ge(ym_read, k + 1 + XR)
                    order.then(dve.tensor_scalar(yscr, rows, 0.0, None, ALU.min))
                    order.then(dve.scalar_tensor_tensor(out=rows, in0=rows, scalar=0.0, in1=yscr, op0=ALU.max, op1=ALU.add))
                    order.did(dve.tensor_scalar(yscr, rows, 1e4, -1e4, ALU.min, ALU.max))
                    last = order.did(dve.tensor_scalar(bad, rows, 0.0, 0.0, ALU.mult, ALU.not_equal))
                    wait_apart(dve, s_dve4, order.base + last)
                    dve.copy_predicated(out=rows, mask=bad, data=yscr).then_inc(ym_ready, 1)

                def weights(which):
                    dve.wait_ge(w_in, (pair * 2 + which + 1) * 48)
                    order.then(dve.tensor_copy(w1p[:, which, 0, :], w1s))
                    order.then(dve.tensor_tensor(w1p[:, which, 1, :], w1s, w1p[:, which, 0, :].bitcast(F32), ALU.subtract))
                    dve.sem_inc(w_free, 1)
                    dve.sem_inc(w_ready, 1)

                parts(0)
                parts(1)
                weights(0)
                for c in range(2 * CH):
                    k = pair * (2 * CH) + c
                    e = pair * 2 + c // CH
                    if c == CH - 1:
                        weights(1)
                    dve.wait_ge(hid_full, (k + 1) * 2)
                    dve.tensor_scalar(hid[:, c % 2, 1, :], ps_s[:, 2 * (c % 2) + 1, :],
                                      b1c[:, bass.ds(e, 1), 1:2].rearrange("p a b -> p (a b)"), 0.0,
                                      ALU.add, ALU.max).then_inc(hid_b, 1)
                    if c + 2 < 2 * CH:
                        parts(c + 2)
                    if c >= 1:
                        to_add(c - 1)
                to_add(2 * CH - 1)
                assert order.n == ND4, order.n


_INS = ['x', 'L0_tok_conv1_w', 'L0_tok_conv1_b', 'L0_tok_bn_gamma', 'L0_tok_bn_beta', 'L0_tok_bn_mean',
        'L0_tok_bn_var', 'L0_tok_conv2_w', 'L0_tok_conv2_b', 'L0_attn_Wq', 'L0_attn_bq', 'L0_attn_Wk', 'L0_attn_bk',
        'L0_attn_Wv', 'L0_attn_bv', 'L0_attn_Wo', 'L0_attn_bo', 'L0_ffn_gate_w', 'L0_ffn_gate_b', 'L0_ffn_w1',
        'L0_ffn_b1', 'L0_ffn_w2', 'L0_ffn_b2']


def kernel(**inputs):
    import concourse.bacc as _bacc
    from concourse.bass_utils import run_bass_kernel_spmd as _run

    nc = _bacc.Bacc("TRN2", target_bir_lowering=False, num_devices=1)
    arrays, args = {}, []
    for name in _INS:
        a = np.ascontiguousarray(inputs[name])
        arrays[f"in_{name}"] = a
        args.append(nc.dram_tensor(f"in_{name}", a.shape, mybir.dt.from_np(a.dtype), kind="ExternalInput").ap())
    b, c, hh, ww = inputs['x'].shape
    slots = -(-5 * b * c * hh // 4)
    args.append(nc.dram_tensor("out_0", (b, c * hh, ww), F32, kind="ExternalOutput").ap())
    args.append(nc.dram_tensor("slots_x", (slots, ww + 2), F32).ap())
    tower(nc, *args)
    r = _run(nc, [arrays], core_ids=[0])
    return r.results[0]["out_0"]
```
